# Optimizing a Trainium2 kernel written in Bass

```python
import numpy as np
import jax
import jax.numpy as jnp

def _softmax(x, axis=-1):
    return jax.nn.softmax(x, axis=axis)

def _gelu(x):
    return jax.nn.gelu(x, approximate=True)

def _silu(x):
    return jax.nn.silu(x)

def _sigmoid(x):
    return jax.nn.sigmoid(x)

def _layernorm(x, axis=-1, eps=1e-05):
    m = jnp.mean(x, axis=axis, keepdims=True)
    v = jnp.var(x, axis=axis, keepdims=True)
    return (x - m) / jnp.sqrt(v + eps)

def _scatter_add(tgt, idx, src, axis=0):
    return tgt.at[idx].add(src)

def _segment_sum(src, seg, n):
    return jax.ops.segment_sum(src, seg, n)
kernel_name = 'mk_seq_preln_d1_jaxref_r8_dc8236'

def setup_inputs(seed: int=0):
    np.random.seed(seed)
    _w = jnp.asarray

    def _L0_attn_setup():
        import jax, jax.numpy as jnp
        import numpy as np
        B, S, D = (8, 256, 128)
        key = jax.random.key(seed)
        kx, kw, kb = jax.random.split(key, 3)
        x = jax.random.normal(kx, (B, S, D), dtype=jnp.float32)
        W = jax.random.normal(kw, (3 * D, D), dtype=jnp.float32) * (1.0 / np.sqrt(D))
        b = jax.random.normal(kb, (3 * D,), dtype=jnp.float32) * 0.01
        return {'x': x, 'W': W, 'b': b}
    _L0_attn_in = _L0_attn_setup()

    def _L0_ffn_setup():
        import jax, jax.numpy as jnp
        import numpy as np
        EPS = 1e-08

        def _ternary_linear(x, w):
            alpha = jnp.mean(jnp.abs(w))
            w_t = jnp.sign(w) * (jnp.abs(w) > 0.5 * alpha).astype(w.dtype)
            w_q = w + jax.lax.stop_gradient(w_t - w)
            d = x.shape[-1]
            rms = jnp.sqrt(jnp.sum(x * x, axis=-1, keepdims=True)) / jnp.sqrt(jnp.asarray(d, x.dtype))
            x_norm = x / (rms + EPS)
            return jnp.einsum('bsd,fd->bsf', x_norm, w_q)
        key = jax.random.key(seed)
        k1, k2, k3 = jax.random.split(key, 3)
        d_model, d_ff = (128, 512)
        B, S = (4, 512)
        x = jax.random.normal(k1, (B, S, d_model), dtype=jnp.float32)
        w_up = jax.random.normal(k2, (d_ff, d_model), dtype=jnp.float32) * 0.02
        w_down = jax.random.normal(k3, (d_model, d_ff), dtype=jnp.float32) * 0.02
        return {'x': x, 'w_up': w_up, 'w_down': w_down}
    _L0_ffn_in = _L0_ffn_setup()
    _d = {'L0_attn_x': _L0_attn_in['x'], 'L0_attn_W': _L0_attn_in['W'], 'L0_attn_b': _L0_attn_in['b'], 'L0_ffn_w_up': _L0_ffn_in['w_up'], 'L0_ffn_w_down': _L0_ffn_in['w_down']}
    _x0 = _d['L0_attn_x']
    _d['L0_attn_x'] = jax.random.normal(jax.random.fold_in(jax.random.key(seed), 1), (8, 512, 128), dtype=_x0.dtype)
    del _x0
    return _d

def reference(L0_attn_x, L0_attn_W, L0_attn_b, L0_ffn_w_up, L0_ffn_w_down):

    def _L0_attn_ref(x, W, b):
        import jax, jax.numpy as jnp
        import numpy as np
        B, S, D = (8, 256, 128)
        qkv = jnp.einsum('bsd,fd->bsf', x, W) + b
        q, k, v = jnp.split(qkv, 3, axis=-1)
        attn = jnp.einsum('bik,bjk->bij', q, k) / k.shape[-1]
        attn = jax.nn.softmax(attn, axis=1)
        out = jnp.einsum('bij,bjk->bik', attn, v)
        return out

    def _L0_ffn_ref(x, w_up, w_down):
        import jax, jax.numpy as jnp
        import numpy as np
        EPS = 1e-08

        def _ternary_linear(x, w):
            alpha = jnp.mean(jnp.abs(w))
            w_t = jnp.sign(w) * (jnp.abs(w) > 0.5 * alpha).astype(w.dtype)
            w_q = w + jax.lax.stop_gradient(w_t - w)
            d = x.shape[-1]
            rms = jnp.sqrt(jnp.sum(x * x, axis=-1, keepdims=True)) / jnp.sqrt(jnp.asarray(d, x.dtype))
            x_norm = x / (rms + EPS)
            return jnp.einsum('bsd,fd->bsf', x_norm, w_q)
        h = jax.nn.gelu(_ternary_linear(x, w_up), approximate=False)
        return _ternary_linear(h, w_down)
    x = L0_attn_x
    x = x + _L0_attn_ref(_layernorm(x, axis=-1), L0_attn_W, L0_attn_b)
    x = x + _L0_ffn_ref(_layernorm(x, axis=-1), L0_ffn_w_up, L0_ffn_w_down)
    return x

_drawn_inputs = setup_inputs


def setup_inputs(seed=0):
    import zlib

    import numpy as np

    out = dict(_drawn_inputs(seed))
    spreads = {}
    factors = {'L0_attn_b': 5.28}
    for name, (base, spread) in spreads.items():
        noise = np.random.default_rng([zlib.crc32(name.encode()), seed]).standard_normal(out[name].shape)
        drawn = base * np.exp(spread * noise) if base else spread * noise
        out[name] = jnp.asarray(drawn.astype(out[name].dtype))
    for name, factor in factors.items():
        out[name] = (out[name] * factor).astype(out[name].dtype)
    return out
```

```python
from contextlib import ExitStack

import concourse.bass as bass
from concourse import mybir

P = 128
F32 = mybir.dt.float32
F16 = mybir.dt.float16
ALU = mybir.AluOpType
ACT = mybir.ActivationFunctionType
AX = mybir.AxisListType

LN_EPS = 1e-5
RMS_EPS = 1e-8

S_N = 2.0**12
S_W = 2.0**12
S_M = 2.0**8
S_P = 2.0**12
S_V = 2.0**8
S_H = 2.0**8
LN_S_P = 8.317766166719343


def build(nc, x_d, w_d, bcol_d, bv_d, wup_d, wdn_d, out_d):
    GROUPS, TOKENS, D = x_d.shape
    F = wup_d.shape[1]
    TILES = TOKENS // P
    FC = F // P
    assert D == P and w_d.shape == (P, 3, D) and FC == 4 and TILES == 4 and GROUPS == 8

    x_v = x_d.rearrange("g (p t) d -> g p (t d)", t=TILES)
    out_v = out_d.rearrange("g (p t) d -> g p (t d)", t=TILES)

    with ExitStack() as ctx:
        def sb(name, shape, dt=F32):
            return ctx.enter_context(nc.sbuf_tensor(name, shape, dt))

        def psum(name, shape, dt=F32):
            return ctx.enter_context(nc.psum_tensor(name, shape, dt))

        def sem(name):
            return ctx.enter_context(nc.semaphore(name))

        x = sb("x", [P, GROUPS, TILES * D])
        w_nat = sb("w_nat", [P, 3, D])
        b_col = sb("b_col", [P, 3])
        b_v = sb("b_v", [P, D])
        bk_sel = sb("bk_sel", [P, P])
        ffn_w = sb("ffn_w", [P, 2, F])
        part = sb("part", [P, P])
        b_abs = sb("b_abs", [P, 3])
        mcol = sb("mcol", [P, 1])
        diag = sb("diag", [P, 4])
        tot = sb("tot", [P, 8])
        rcp = sb("rcp", [P, 4])
        akq = sb("akq", [P, 1])
        scl = sb("scl", [P, 8])
        ident = sb("ident", [P, P])
        ones = sb("ones", [P, P])
        big = sb("big", [P, TOKENS], F16)
        m_hi = sb("m_hi", [P, P], F16)
        m_lo = sb("m_lo", [P, P], F16)
        wv_hi = sb("wv_hi", [P, P], F16)
        wv_lo = sb("wv_lo", [P, P], F16)
        c_hi = sb("c_hi", [P, P], F16)
        c_lo = sb("c_lo", [P, P], F16)
        c_mix = sb("c_mix", [P, P], F16)
        bv_hi = sb("bv_hi", [P, P], F16)
        bv_lo = sb("bv_lo", [P, P], F16)
        bv_mix = sb("bv_mix", [P, P], F16)
        t_gt = sb("t_gt", [P, 2, F], F16)
        t_lt = sb("t_lt", [P, 2, F], F16)
        tern = sb("tern", [P, 2, F], F16)
        xs = sb("xs", [P, 2, TILES * D])
        bn = sb("bn", [P, 2, TILES, 6])
        mv = sb("mv", [P, 2, TILES, 2])
        nmean = sb("nmean", [P, 2, TILES])
        var2 = sb("var2", [P, 2, 2, TILES])
        root = sb("root", [P, 2, 2, TILES])
        epsroot = sb("epsroot", [P, 2, TILES])
        den = sb("den", [P, 2, TILES])
        rstd = sb("rstd", [P, 2, TILES])
        p_half = sb("p_half", [P, 2, TILES])
        m_half = sb("m_half", [P, TILES])
        xn = sb("xn", [P, 2, TILES * D])
        xT_hi = sb("xT_hi", [P, 2, TOKENS], F16)
        xT_lo = sb("xT_lo", [P, 2, TOKENS], F16)
        kq_hi = sb("kq_hi", [P, TOKENS], F16)
        kq_lo = sb("kq_lo", [P, TOKENS], F16)
        nmax = sb("nmax", [P, TILES])
        nbias = sb("nbias", [P, TILES])
        prob = sb("prob", [P, TILES, TOKENS])
        p_hi = sb("p_hi", [P, 2, TILES, TOKENS], F16)
        p_lo = sb("p_lo", [P, 2, TILES, TOKENS], F16)
        psums = sb("psums", [P, TILES])
        rsums = sb("rsums", [P, TILES])
        v_s = sb("v_s", [P, TILES, D])
        v_hi = sb("v_hi", [P, 2, TILES, D], F16)
        v_lo = sb("v_lo", [P, 2, TILES, D], F16)
        h = sb("h", [P, FC, TOKENS])
        h_hi = sb("h_hi", [P, 2, FC, TOKENS], F16)
        h_lo = sb("h_lo", [P, 2, FC, TOKENS], F16)
        sq = sb("sq", [P, FC, TOKENS])
        sqs = sb("sqs", [P, 2, TOKENS])
        meansq = sb("meansq", [P, TILES])
        rms = sb("rms", [P, TILES])
        rmsd = sb("rmsd", [P, TILES])
        rrms = sb("rrms", [P, TILES])

        psT = psum("psT", [P, TOKENS])
        psV = psum("psV", [P, TILES, D])
        psS = [psum(f"psS{i}", [P, TOKENS]) for i in range(4)]
        psO = psum("psO", [P, TILES, D])
        psQ = psum("psQ", [P, TOKENS])
        psW = psQ

        w_loaded = sem("w_loaded")
        bcol_loaded = sem("bcol_loaded")
        bv_loaded = sem("bv_loaded")
        up_loaded = sem("up_loaded")
        dn_loaded = sem("dn_loaded")
        x_loaded = sem("x_loaded")
        xs_loaded = [sem("xs_loaded_even"), sem("xs_loaded_odd")]
        consts_ready = sem("consts_ready")
        ident_ready = sem("ident_ready")
        prep = sem("prep")
        pe_prep = sem("pe_prep")
        act_prep = sem("act_prep")
        bn_done = sem("bn_done")
        stats_ready = sem("stats_ready")
        pool_a = sem("pool_a")
        pool_b = sem("pool_b")
        den_ready = sem("den_ready")
        rstd_ready = sem("rstd_ready")
        xn_ready = sem("xn_ready")
        t_done = sem("t_done")
        xhi_ready = sem("xhi_ready")
        xlo_ready = sem("xlo_ready")
        k_done = sem("k_done")
        kqhi_ready = sem("kqhi_ready")
        kqlo_ready = sem("kqlo_ready")
        v_done = sem("v_done")
        scores_done = sem("scores_done")
        max_done = sem("max_done")
        bias_ready = sem("bias_ready")
        exp_done = sem("exp_done")
        phi_ready = sem("phi_ready")
        plo_ready = sem("plo_ready")
        rsum_ready = sem("rsum_ready")
        vs_ready = sem("vs_ready")
        vhi_ready = sem("vhi_ready")
        vlo_ready = sem("vlo_ready")
        pv_done = sem("pv_done")
        x2_ready = sem("x2_ready")
        up_done = sem("up_done")
        gelu_done = sem("gelu_done")
        hhi_act = sem("hhi_act")
        hhi_dve = sem("hhi_dve")
        hlo_ready = sem("hlo_ready")
        sq_ready = sem("sq_ready")
        sqs_ready = sem("sqs_ready")
        q_done = sem("q_done")
        meansq_ready = sem("meansq_ready")
        rms_ready = sem("rms_ready")
        rmsd_ready = sem("rmsd_ready")
        rrms_ready = sem("rrms_ready")
        down_done = sem("down_done")
        x3_ready = sem("x3_ready")
        stored = sem("stored")
        pool_gate = sem("pool_gate")
        dve_gate = sem("dve_gate")
        sp_gate = sem("sp_gate")

        EXP_SCALE, OUT_SCALE, M_SCALE, V_SCALE, T_UP, T_DN, NT_UP, NT_DN = range(8)

        A_END, B_END = GROUPS, 2 * GROUPS
        LOOPS = ((2, 6), (GROUPS + 1, GROUPS + 5))

        def after_first(g, i):
            return g >= 1 or not isinstance(i, int)

        def run_steps(eng, step):
            s = 0
            while s <= B_END:
                loop = [b for a, b in LOOPS if a == s]
                if loop:
                    with eng.Fori(0, loop[0] - s - 1, 2) as i:
                        step(s, i)
                        step(s + 1, i)
                    s = loop[0]
                else:
                    step(s, 0)
                    s += 1

        HI_ON_ACT = (0, 2)

        block = ctx.enter_context(nc.Block())

        @block.sync
        def _(sp):
            sp.dma_start(w_nat[:, :, :], w_d).then_inc(w_loaded, 16)
            sp.dma_start(xs[:, 0, :], x_v[0]).then_inc(xs_loaded[0], 16)
            sp.dma_start(xs[:, 1, :], x_v[1]).then_inc(xs_loaded[1], 16)
            sp.dma_start(x[:, :, :], x_d.rearrange("g (p t) d -> p g (t d)", t=TILES)).then_inc(x_loaded, 16)
            with sp.Fori(2, GROUPS - 1, 2) as i:
                for u in range(2):
                    sp.wait_ge(xn_ready, i + u - 1)
                    sp.sem_inc(sp_gate, 1)
                    sp.dma_start(xs[:, u, :], x_v[bass.ds(i + u, 1)].rearrange("g p n -> p (g n)")
                                 ).then_inc(xs_loaded[u], 16)
            with sp.Fori(0, GROUPS - 1, 2) as i:
                for u in range(2):
                    sp.wait_ge(xn_ready, i + u + GROUPS - 1)
                    sp.sem_inc(sp_gate, 1)
                    sp.wait_ge(x2_ready, i + u + 1)
                    sp.sem_inc(sp_gate, 1)
                    sp.dma_start(xs[:, u, :], x[:, bass.ds(i + u, 1), :].rearrange("p g n -> p (g n)")
                                 ).then_inc(xs_loaded[u], 16)
            with sp.Fori(0, GROUPS, 1) as i:
                sp.wait_ge(x3_ready, i + 2)
                sp.dma_start(out_v[bass.ds(i, 1)].rearrange("g p n -> p g n"),
                             x[:, bass.ds(i, 1), :]).then_inc(stored, 16)
            sp.wait_ge(stored, 16 * GROUPS)

        @block.scalar
        def _(act):
            act.dma_start(b_col[:, :], bcol_d).then_inc(bcol_loaded, 16)
            act.wait_ge(consts_ready, 1)
            for row in (0, 64):
                act.dma_start(b_v[row:row + 1, :], bv_d).then_inc(bv_loaded, 16)
            act.dma_start(ffn_w[:, 0, :], wup_d).then_inc(up_loaded, 16)
            act.dma_start(ffn_w[:, 1, :], wdn_d).then_inc(dn_loaded, 16)

            act.wait_ge(prep, 9)
            act.wait_ge(bv_loaded, 32)
            nc.scalar.activation(bv_hi[:, :], b_v[:, :], ACT.Identity,
                                 scale=scl[:, V_SCALE:V_SCALE + 1]).then_inc(act_prep, 1)
            act.wait_ge(pe_prep, 2)
            nc.scalar.activation(m_hi[:, :], psS[0][:, 0:P], ACT.Identity,
                                 scale=scl[:, M_SCALE:M_SCALE + 1])
            nc.scalar.activation(c_hi[:, :], psS[0][:, P:2 * P], ACT.Identity,
                                 scale=scl[:, M_SCALE:M_SCALE + 1])
            nc.scalar.activation(wv_hi[:, :], w_nat[:, 2, :], ACT.Identity,
                                 scale=scl[:, V_SCALE:V_SCALE + 1]).then_inc(act_prep, 1)

            def x_head(n, i):
                act.wait_ge(t_done, n + 1 + i)
                nc.scalar.copy(xT_hi[:, n % 2, :], psT[:, :]).then_inc(xhi_ready, 1)

            def kq_head(n, i):
                act.wait_ge(k_done, n + 1 + i)
                nc.scalar.mul(kq_hi[:, :], psT[:, :], 1.0 / (S_N * S_M)).then_inc(kqhi_ready, 1)

            def exp(s, i, j):
                act.wait_ge(bias_ready, 4 * (s + i) + j + 1)
                if s >= 1:
                    act.wait_ge(plo_ready, 4 * (s - 1 + i) + j + 1)
                    if j == 0:
                        act.wait_ge(rsum_ready, s + i)
                nc.scalar.activation(prob[:, j, :], psS[j][:, :], ACT.Exp, bias=nbias[:, j:j + 1],
                                     scale=scl[:, EXP_SCALE:EXP_SCALE + 1],
                                     accum_out=psums[:, j:j + 1]).then_inc(exp_done, 1)

            def p_head(s, i, j):
                act.wait_ge(exp_done, 4 * (s + i) + j + 1)
                nc.scalar.copy(p_hi[:, s % 2, j, :], prob[:, j, :]).then_inc(phi_ready, 1)

            def v_head(s, i):
                act.wait_ge(vs_ready, s + 1 + i)
                nc.scalar.copy(v_hi[:, s % 2, :, :], v_s[:, :, :]).then_inc(vhi_ready, 1)

            def gelu(s, i, c):
                g = s - GROUPS
                act.wait_ge(up_done, 4 * (g + i) + c + 1)
                if g >= 1:
                    act.wait_ge(hlo_ready, 4 * (g - 1 + i) + c + 1)
                nc.scalar.activation(h[:, c, :], psS[c][:, :], ACT.Gelu, scale=1.0 / S_N).then_inc(gelu_done, 1)

            def h_head_and_square(s, i, c):
                g = s - GROUPS
                act.wait_ge(gelu_done, 4 * (g + i) + c + 1)
                if c in HI_ON_ACT:
                    nc.scalar.mul(h_hi[:, s % 2, c, :], h[:, c, :], S_H).then_inc(hhi_act, 1)
                if g >= 1 and c % 2 == 0:
                    act.wait_ge(sqs_ready, 2 * (g - 1 + i) + c // 2 + 1)
                nc.scalar.square(sq[:, c, :], h[:, c, :]).then_inc(sq_ready, 1)

            def step(s, i):
                if s == 0:
                    x_head(0, 0)
                    kq_head(0, 0)
                if s + 1 < B_END:
                    x_head(s + 1, i)
                if s < A_END:
                    exp(s, i, 0)
                    exp(s, i, 1)
                    p_head(s, i, 0)
                    exp(s, i, 2)
                    p_head(s, i, 1)
                    if s + 1 < A_END:
                        kq_head(s + 1, i)
                    exp(s, i, 3)
                    p_head(s, i, 2)
                    p_head(s, i, 3)
                    v_head(s, i)
                elif s < B_END:
                    gelu(s, i, 0)
                    for c in range(1, FC):
                        gelu(s, i, c)
                        h_head_and_square(s, i, c - 1)
                    h_head_and_square(s, i, FC - 1)

            run_steps(act, step)

        @block.gpsimd
        def _(pool):
            nc.gpsimd.memset(b_v[:, :], 0.0).then_inc(consts_ready, 1)
            nc.gpsimd.memset(p_half[:, :, :], 0.5)
            nc.gpsimd.memset(m_half[:, :], -0.5).then_inc(pool_b, 1)
            nc.gpsimd.memset(ident[:, :], 0.0).then_inc(pool_a, 1)
            pool.wait_ge(pool_a, 1)
            nc.gpsimd.affine_select(out=ident[:, :], in_=ident[:, :], compare_op=ALU.not_equal, fill=1.0,
                                    base=0, pattern=[[-1, P]], channel_multiplier=1).then_inc(ident_ready, 1)
            pool.wait_ge(pool_b, 1)

            def normalise(n, i):
                u = n % 2
                attn = n < GROUPS
                pool.wait_ge(stats_ready, n + 1 + i)
                pool.sem_inc(pool_gate, 1)
                mean = mv[:, u, :, 0]
                var = mv[:, u, :, 1]
                nc.gpsimd.tensor_scalar(nmean[:, u, :], mean, -1.0, 1.0, ALU.mult, ALU.mult)
                if attn:
                    nc.gpsimd.tensor_scalar(var2[:, u, 0, :], var, LN_EPS, S_N**-2, ALU.add,
                                            ALU.mult).then_inc(pool_a, 1)
                    pool.wait_ge(pool_a, n + 2 + i)
                    nc.gpsimd.tensor_tensor(rstd[:, u, :], var2[:, u, 0, :], m_half[:, :],
                                            ALU.pow).then_inc(pool_b, 1)
                else:
                    nc.gpsimd.tensor_scalar(var2[:, u, 0, :], var, 1.0, 1.0, ALU.mult, ALU.mult)
                    nc.gpsimd.tensor_scalar(var2[:, u, 1, :], var, LN_EPS, 1.0, ALU.add,
                                            ALU.mult).then_inc(pool_a, 1)
                    pool.wait_ge(pool_a, n + 2 + i)
                    nc.gpsimd.tensor_tensor(root[:, u, :, :], var2[:, u, :, :], p_half[:, :, :],
                                            ALU.pow).then_inc(pool_b, 1)
                    pool.wait_ge(pool_b, n + 2 + i)
                    pool.sem_inc(pool_gate, 1)
                    nc.gpsimd.tensor_scalar(epsroot[:, u, :], root[:, u, 1, :], RMS_EPS / S_N, 1.0,
                                            ALU.mult, ALU.mult)
                    nc.gpsimd.tensor_scalar(den[:, u, :], root[:, u, 0, :], 1.0 / S_N, 1.0,
                                            ALU.mult, ALU.mult).then_inc(den_ready, 1)
                if attn:
                    apply_norm(n, i)

            def apply_norm(n, i):
                u = n % 2
                if n >= 2:
                    pool.wait_ge(t_done, n - 1 + i)
                if n >= GROUPS:
                    pool.wait_ge(rstd_ready, n - GROUPS + 1 + i)
                else:
                    pool.wait_ge(pool_b, n + 2 + i)
                pool.sem_inc(pool_gate, 1)
                for t in range(TILES):
                    last = nc.gpsimd.tensor_scalar(xn[:, u, t * D:(t + 1) * D], xs[:, u, t * D:(t + 1) * D],
                                                   nmean[:, u, t:t + 1], rstd[:, u, t:t + 1], ALU.add, ALU.mult)
                last.then_inc(xn_ready, 1)

            def p_rest(s, i, j):
                pool.wait_ge(phi_ready, 4 * (s + i) + j + 1)
                nc.gpsimd.tensor_tensor(p_lo[:, s % 2, j, :], prob[:, j, :], p_hi[:, s % 2, j, :],
                                        ALU.subtract).then_inc(plo_ready, 1)

            def add_squares(s, i, k):
                g = s - GROUPS
                pool.wait_ge(sq_ready, 4 * (g + i) + 2 * k + 2)
                if g >= 1 and k == 0:
                    pool.wait_ge(q_done, g + i)
                nc.gpsimd.tensor_tensor(sqs[:, k, :], sq[:, 2 * k, :], sq[:, 2 * k + 1, :],
                                        ALU.add).then_inc(sqs_ready, 1)

            def root_meansq(s, i):
                g = s - GROUPS
                pool.wait_ge(meansq_ready, g + 2 + i)
                nc.gpsimd.tensor_tensor(rms[:, :], meansq[:, :], p_half[:, 0, :], ALU.pow).then_inc(rms_ready, 1)

            def step(s, i):
                if s == 0:
                    normalise(0, 0)
                    normalise(1, 0)
                if s + 2 < B_END:
                    normalise(s + 2, i)
                if s < A_END:
                    p_rest(s, i, 0)
                    p_rest(s, i, 1)
                    if GROUPS <= s + 2:
                        apply_norm(s + 2, i)
                    p_rest(s, i, 2)
                    p_rest(s, i, 3)
                elif s < B_END:
                    add_squares(s, i, 0)
                    if s + 2 < B_END:
                        apply_norm(s + 2, i)
                    if s > A_END:
                        root_meansq(s - 1, i)
                    add_squares(s, i, 1)
                else:
                    root_meansq(s - 1, i)

            run_steps(pool, step)

        @block.vector
        def _(dve):
            def x_at(n, i):
                slot = n % GROUPS
                if isinstance(i, int):
                    return x[:, slot + i, :]
                return x[:, bass.ds(slot + i, 1), :].rearrange("p a n -> p (a n)")

            def token_stats(n, i):
                u = n % 2
                dve.wait_ge(xs_loaded[u], 16 * (n // 2) + 16 + 8 * i)
                for t in range(TILES):
                    last = nc.vector.bn_stats(bn[:, u, t, :], xs[:, u, t * D:(t + 1) * D])
                last.then_inc(bn_done, 1)

            def combine_stats(n, i):
                u = n % 2
                if n >= 2:
                    dve.wait_ge(xn_ready, n - 1 + i)
                dve.wait_ge(bn_done, n + 1 + i)
                dve.sem_inc(dve_gate, 1)
                for t in range(TILES):
                    last = nc.vector.bn_aggr(mv[:, u, t, :], bn[:, u, t, :])
                last.then_inc(stats_ready, 1)

            def stats(n, i):
                token_stats(n, i)
                combine_stats(n, i)

            dve.sem_inc(meansq_ready, 1)
            dve.sem_inc(rms_ready, 1)
            dve.sem_inc(x3_ready, 1)
            nc.vector.memset(part[:, :], 0.0)
            nc.vector.memset(ones[:, :], 1.0)
            nc.vector.memset(big[:, :], S_N)
            nc.vector.memset(bk_sel[:, :], 0.0)
            nc.vector.memset(c_mix[:, :], 0.0)
            nc.vector.memset(bv_mix[:, :], 0.0).then_inc(prep, 1)
            dve.wait_ge(prep, 1)
            dve.wait_ge(bcol_loaded, 16)
            nc.vector.tensor_scalar(b_abs[:, :], b_col[:, :], -1.0, None, ALU.mult)
            nc.vector.tensor_copy(bk_sel[:, 0:1], b_col[:, 1:2])
            nc.vector.tensor_copy(bk_sel[:, 64:65], b_col[:, 1:2])
            dve.wait_ge(w_loaded, 16)
            nc.vector.tensor_reduce(part[:, 0:3], w_nat[:, :, :], AX.X, ALU.max,
                                    apply_absolute_value=True).then_inc(prep, 1)
            dve.wait_ge(prep, 2)
            nc.vector.tensor_tensor(b_abs[:, :], b_abs[:, :], b_col[:, :], ALU.max).then_inc(prep, 1)
            dve.wait_ge(prep, 3)
            nc.vector.tensor_tensor(part[:, 0:3], part[:, 0:3], b_abs[:, :], ALU.max)
            dve.wait_ge(up_loaded, 16)
            nc.vector.tensor_reduce(part[:, 3:4], ffn_w[:, 0, :], AX.X,
                                    ALU.add, apply_absolute_value=True)
            dve.wait_ge(dn_loaded, 16)
            nc.vector.tensor_reduce(part[:, 4:5], ffn_w[:, 1, :], AX.X,
                                    ALU.add, apply_absolute_value=True).then_inc(prep, 1)
            stats(0, 0)
            dve.wait_ge(pe_prep, 1)
            nc.vector.reduce_max(mcol[:, :], psW[:, 0:P], AX.X).then_inc(prep, 1)
            dve.wait_ge(prep, 5)
            nc.vector.tensor_scalar(diag[:, 0:3], ident[:, 0:3], mcol[:, 0:1], None, ALU.mult).then_inc(prep, 1)
            stats(1, 0)
            dve.wait_ge(pe_prep, 2)
            nc.vector.tensor_scalar(tot[:, 0:3], psW[:, P:P + 3], 1e-30, None, ALU.max)
            nc.vector.tensor_scalar(scl[:, T_UP:T_DN + 1], psW[:, P + 3:P + 5], 0.5 / (F * D), None, ALU.mult)
            nc.vector.tensor_scalar(scl[:, NT_UP:NT_DN + 1], psW[:, P + 3:P + 5], -0.5 / (F * D), None,
                                    ALU.mult).then_inc(prep, 1)
            dve.wait_ge(prep, 7)
            nc.vector.reciprocal(rcp[:, 0:3], tot[:, 0:3])
            nc.vector.tensor_scalar(scl[:, EXP_SCALE:EXP_SCALE + 1], tot[:, 0:1], tot[:, 1:2],
                                    1.0 / (D * S_N), ALU.mult, ALU.mult)
            nc.vector.tensor_scalar(scl[:, OUT_SCALE:OUT_SCALE + 1], tot[:, 2:3], 1.0 / (S_P * S_V), None,
                                    ALU.mult).then_inc(prep, 1)
            dve.wait_ge(prep, 8)
            nc.vector.tensor_scalar(scl[:, M_SCALE:M_SCALE + 1], rcp[:, 0:1], rcp[:, 1:2], S_M, ALU.mult, ALU.mult)
            nc.vector.tensor_scalar(scl[:, V_SCALE:V_SCALE + 1], rcp[:, 2:3], S_W, None,
                                    ALU.mult).then_inc(prep, 1)
            dve.wait_ge(prep, 9)
            dve.wait_ge(act_prep, 1)
            nc.vector.scalar_tensor_tensor(out=bv_lo[:, :], in0=b_v[:, :], scalar=scl[:, V_SCALE:V_SCALE + 1],
                                           in1=bv_hi[:, :], op0=ALU.mult, op1=ALU.subtract)
            dve.wait_ge(act_prep, 2)
            nc.vector.scalar_tensor_tensor(out=m_lo[:, :], in0=psS[0][:, 0:P], scalar=scl[:, M_SCALE:M_SCALE + 1],
                                           in1=m_hi[:, :], op0=ALU.mult, op1=ALU.subtract)
            nc.vector.scalar_tensor_tensor(out=c_lo[:, :], in0=psS[0][:, P:2 * P],
                                           scalar=scl[:, M_SCALE:M_SCALE + 1],
                                           in1=c_hi[:, :], op0=ALU.mult, op1=ALU.subtract)
            nc.vector.scalar_tensor_tensor(out=wv_lo[:, :], in0=w_nat[:, 2, :],
                                           scalar=scl[:, V_SCALE:V_SCALE + 1],
                                           in1=wv_hi[:, :], op0=ALU.mult, op1=ALU.subtract).then_inc(prep, 1)
            dve.wait_ge(prep, 10)
            nc.vector.tensor_copy(c_mix[0:1, :], c_hi[0:1, :])
            nc.vector.tensor_copy(c_mix[64:65, :], c_lo[64:65, :])
            nc.vector.tensor_copy(bv_mix[0:1, :], bv_hi[0:1, :])
            nc.vector.tensor_copy(bv_mix[64:65, :], bv_lo[64:65, :]).then_inc(prep, 1)
            stats(2, 0)

            def ternary_weights():
                for k in range(2):
                    src = ffn_w[:, k, :]
                    nc.vector.tensor_scalar(t_gt[:, k, :], src, scl[:, T_UP + k:T_UP + k + 1], None, ALU.is_gt)
                    last = nc.vector.tensor_scalar(t_lt[:, k, :], src, scl[:, NT_UP + k:NT_UP + k + 1], None,
                                                   ALU.is_lt)
                last.then_inc(prep, 1)
                dve.wait_ge(prep, 12)
                nc.vector.tensor_tensor(tern[:, :, :], t_gt[:, :, :], t_lt[:, :, :],
                                        ALU.subtract).then_inc(prep, 1)

            def x_rest(n, i):
                dve.wait_ge(xhi_ready, n + 1 + i)
                nc.vector.scalar_tensor_tensor(out=xT_lo[:, n % 2, :], in0=psT[:, :], scalar=1.0,
                                               in1=xT_hi[:, n % 2, :], op0=ALU.mult,
                                               op1=ALU.subtract).then_inc(xlo_ready, 1)

            def kq_rest(n, i):
                dve.wait_ge(kqhi_ready, n + 1 + i)
                nc.vector.scalar_tensor_tensor(out=kq_lo[:, :], in0=psT[:, :], scalar=1.0 / (S_N * S_M),
                                               in1=kq_hi[:, :], op0=ALU.mult,
                                               op1=ALU.subtract).then_inc(kqlo_ready, 1)

            def maximum(s, i, j):
                n = 4 * (s + i) + j + 1
                dve.wait_ge(scores_done, n)
                nc.vector.tensor_reduce(nmax[:, j:j + 1], psS[j][:, :], AX.X, ALU.max,
                                        negate=True).then_inc(max_done, 1)

            def exp_bias(s, i, j):
                n = 4 * (s + i) + j + 1
                dve.wait_ge(max_done, n)
                nc.vector.tensor_scalar(nbias[:, j:j + 1], nmax[:, j:j + 1], scl[:, EXP_SCALE:EXP_SCALE + 1],
                                        LN_S_P, ALU.mult, ALU.add).then_inc(bias_ready, 1)

            def divide_values(s, i):
                dve.wait_ge(exp_done, 4 * (s + i) + 4)
                nc.vector.reciprocal(rsums[:, :], psums[:, :]).then_inc(rsum_ready, 1)
                dve.wait_ge(rsum_ready, s + 1 + i)
                dve.wait_ge(v_done, s + 1 + i)
                nc.vector.scalar_tensor_tensor(
                    out=v_s[:, :, :], in0=psV[:, :, :], scalar=S_V * S_P / (S_N * S_W),
                    in1=rsums[:, :].unsqueeze(2).to_broadcast([P, TILES, D]),
                    op0=ALU.mult, op1=ALU.mult).then_inc(vs_ready, 1)

            def v_rest(s, i):
                dve.wait_ge(vhi_ready, s + 1 + i)
                nc.vector.tensor_tensor(v_lo[:, s % 2, :, :], v_s[:, :, :], v_hi[:, s % 2, :, :],
                                        ALU.subtract).then_inc(vlo_ready, 1)

            def add_attention(s, i):
                if s == 0:
                    dve.wait_ge(x_loaded, 16)
                dve.wait_ge(pv_done, s + 1 + i)
                xg = x_at(s, i)
                nc.vector.scalar_tensor_tensor(out=xg, in0=psO[:, :, :].rearrange("p t d -> p (t d)"),
                                               scalar=scl[:, OUT_SCALE:OUT_SCALE + 1], in1=xg,
                                               op0=ALU.mult, op1=ALU.add).then_inc(x2_ready, 1)

            def norm_reciprocal(n, i):
                u = n % 2
                dve.wait_ge(den_ready, n - GROUPS + 1 + i)
                nc.vector.tensor_tensor(den[:, u, :], den[:, u, :], epsroot[:, u, :], ALU.add).then_inc(rmsd_ready, 1)
                dve.wait_ge(rmsd_ready, n - GROUPS + 1 + i)
                nc.vector.reciprocal(rstd[:, u, :], den[:, u, :]).then_inc(rstd_ready, 1)

            def h_head(s, i, c):
                g = s - GROUPS
                dve.wait_ge(gelu_done, 4 * (g + i) + c + 1)
                nc.vector.tensor_scalar(h_hi[:, s % 2, c, :], h[:, c, :], S_H, None, ALU.mult).then_inc(hhi_dve, 1)

            def h_rest(s, i, c):
                g = s - GROUPS
                if c in HI_ON_ACT:
                    dve.wait_ge(hhi_act, len(HI_ON_ACT) * (g + i) + HI_ON_ACT.index(c) + 1)
                else:
                    dve.wait_ge(hhi_dve, (FC - len(HI_ON_ACT)) * (g + i) + c // 2 + 1)
                nc.vector.scalar_tensor_tensor(out=h_lo[:, s % 2, c, :], in0=h[:, c, :], scalar=S_H,
                                               in1=h_hi[:, s % 2, c, :], op0=ALU.mult,
                                               op1=ALU.subtract).then_inc(hlo_ready, 1)

            def mean_square(s, i):
                g = s - GROUPS
                dve.wait_ge(q_done, g + 1 + i)
                if after_first(g, i):
                    dve.wait_ge(rms_ready, g + i + 1)
                nc.vector.tensor_scalar(meansq[:, :], psQ[:, 0:TILES], 1.0 / F, None, ALU.mult).then_inc(meansq_ready, 1)

            def rms_reciprocal(s, i):
                g = s - GROUPS
                dve.wait_ge(rms_ready, g + 2 + i)
                nc.vector.tensor_scalar(rmsd[:, :], rms[:, :], RMS_EPS, S_H, ALU.add, ALU.mult).then_inc(rrms_ready, 1)
                dve.wait_ge(rrms_ready, 2 * (g + i) + 1)
                nc.vector.reciprocal(rrms[:, :], rmsd[:, :]).then_inc(rrms_ready, 1)

            def add_ffn(s, i):
                g = s - GROUPS
                dve.wait_ge(rrms_ready, 2 * (g + i) + 2)
                dve.wait_ge(down_done, g + 1 + i)
                xg = x_at(s, i)
                for t in range(TILES):
                    last = nc.vector.scalar_tensor_tensor(
                        out=xg[:, t * D:(t + 1) * D], in0=psO[:, t, :], scalar=rrms[:, t:t + 1],
                        in1=xg[:, t * D:(t + 1) * D], op0=ALU.mult, op1=ALU.add)
                last.then_inc(x3_ready, 1)

            def step(s, i):
                if s == 0:
                    x_rest(0, 0)
                    kq_rest(0, 0)
                    ternary_weights()
                if s + 1 < B_END:
                    x_rest(s + 1, i)
                if s < A_END:
                    for j in range(TILES):
                        maximum(s, i, j)
                        exp_bias(s, i, j)
                        if j == 1 and s + 2 >= GROUPS:
                            norm_reciprocal(s + 2, i)
                    if s + 1 < A_END:
                        kq_rest(s + 1, i)
                    if s >= 1:
                        add_attention(s - 1, i)
                    if s + 3 < A_END:
                        stats(s + 3, i)
                    divide_values(s, i)
                    if s + 3 >= A_END:
                        stats(s + 3, i)
                    v_rest(s, i)
                elif s < B_END:
                    if s == A_END:
                        add_attention(A_END - 1, 0)
                    h_head(s, i, 1)
                    h_rest(s, i, 0)
                    if s + 2 < B_END:
                        norm_reciprocal(s + 2, i)
                    h_rest(s, i, 1)
                    if s > A_END:
                        mean_square(s - 1, i)
                    h_head(s, i, 3)
                    h_rest(s, i, 2)
                    if s > A_END:
                        rms_reciprocal(s - 1, i)
                    h_rest(s, i, 3)
                    if s > A_END:
                        add_ffn(s - 1, i)
                    if s + 3 < B_END:
                        stats(s + 3, i)
                else:
                    mean_square(s - 1, i)
                    rms_reciprocal(s - 1, i)
                    add_ffn(s - 1, i)

            run_steps(dve, step)

        @block.tensor
        def _(pe):
            pe.wait_ge(prep, 4)
            pe.wait_ge(ident_ready, 1)
            nc.tensor.transpose(psW[:, 0:P], part[:, :], ident[:, :]).then_inc(pe_prep, 1)
            nc.tensor.matmul(psS[0][:, 0:P], w_nat[:, 1, :], w_nat[:, 0, :], start=True, stop=True)
            nc.tensor.matmul(psS[0][:, P:2 * P], bk_sel[:, :], w_nat[:, 0, :], start=True, stop=True)
            pe.wait_ge(prep, 6)
            nc.tensor.matmul(psW[:, P:P + 3], ones[:, :], diag[:, 0:3], start=True, stop=True)
            nc.tensor.matmul(psW[:, P + 3:P + 5], ones[:, :], part[:, 3:5], start=True, stop=True).then_inc(pe_prep, 1)

            def transposes(n, i):
                pe.wait_ge(xn_ready, n + 1 + i)
                if n >= 1:
                    pe.wait_ge(xlo_ready, n + i)
                    if n <= GROUPS:
                        pe.wait_ge(kqlo_ready, n + i)
                for t in range(TILES):
                    last = nc.tensor.transpose(psT[:, t * P:(t + 1) * P], xn[:, n % 2, t * D:(t + 1) * D],
                                               ident[:, :])
                last.then_inc(t_done, 1)

            def project_keys(n, i):
                pe.wait_ge(xlo_ready, n + 1 + i)
                nc.tensor.matmul(psT[:, :], m_hi[:, :], xT_hi[:, n % 2, :], start=True, stop=False)
                nc.tensor.matmul(psT[:, :], m_hi[:, :], xT_lo[:, n % 2, :], start=False, stop=False)
                nc.tensor.matmul(psT[:, :], m_lo[:, :], xT_hi[:, n % 2, :], start=False, stop=False)
                nc.tensor.matmul(psT[:, :], c_mix[:, :], big[:, :], start=False, stop=True).then_inc(k_done, 1)

            def project_values(n, i):
                if n >= 1:
                    pe.wait_ge(vs_ready, n + i)
                for t in range(TILES):
                    hi = xT_hi[:, n % 2, t * P:(t + 1) * P]
                    lo = xT_lo[:, n % 2, t * P:(t + 1) * P]
                    nc.tensor.matmul(psV[:, t, :], hi, wv_hi[:, :], start=True, stop=False)
                    nc.tensor.matmul(psV[:, t, :], hi, wv_lo[:, :], start=False, stop=False)
                    nc.tensor.matmul(psV[:, t, :], lo, wv_hi[:, :], start=False, stop=False)
                    last = nc.tensor.matmul(psV[:, t, :], big[:, 0:P], bv_mix[:, :], start=False, stop=True)
                last.then_inc(v_done, 1)

            def scores(s, i):
                pe.wait_ge(kqlo_ready, s + 1 + i)
                for j in range(TILES):
                    if s >= 1:
                        pe.wait_ge(exp_done, 4 * (s - 1 + i) + j + 1)
                    hi = kq_hi[:, j * P:(j + 1) * P]
                    lo = kq_lo[:, j * P:(j + 1) * P]
                    nc.tensor.matmul(psS[j][:, :], hi, xT_hi[:, s % 2, :], start=True, stop=False)
                    nc.tensor.matmul(psS[j][:, :], hi, xT_lo[:, s % 2, :], start=False, stop=False)
                    nc.tensor.matmul(psS[j][:, :], lo, xT_hi[:, s % 2, :], start=False,
                                     stop=True).then_inc(scores_done, 1)

            def weigh_values(s, i):
                pe.wait_ge(vlo_ready, s + 1 + i)
                pe.wait_ge(plo_ready, 4 * (s + i) + 4)
                if after_first(s, i):
                    pe.wait_ge(x2_ready, s + i)
                u = s % 2
                for t in range(TILES):
                    for j in range(TILES):
                        hi = p_hi[:, u, j, t * P:(t + 1) * P]
                        lo = p_lo[:, u, j, t * P:(t + 1) * P]
                        nc.tensor.matmul(psO[:, t, :], hi, v_hi[:, u, j, :], start=(j == 0), stop=False)
                        nc.tensor.matmul(psO[:, t, :], hi, v_lo[:, u, j, :], start=False, stop=False)
                        last = nc.tensor.matmul(psO[:, t, :], lo, v_hi[:, u, j, :], start=False,
                                                stop=(j == TILES - 1))
                last.then_inc(pv_done, 1)

            def project_up(s, i):
                g = s - GROUPS
                pe.wait_ge(xlo_ready, s + 1 + i)
                for c in range(FC):
                    if g >= 1:
                        pe.wait_ge(gelu_done, 4 * (g - 1 + i) + c + 1)
                    else:
                        pe.wait_ge(exp_done, 4 * (A_END - 1) + c + 1)
                    w = tern[:, 0, c * P:(c + 1) * P]
                    nc.tensor.matmul(psS[c][:, :], w, xT_hi[:, s % 2, :], start=True, stop=False)
                    nc.tensor.matmul(psS[c][:, :], w, xT_lo[:, s % 2, :], start=False,
                                     stop=True).then_inc(up_done, 1)

            def sum_squares(s, i):
                g = s - GROUPS
                pe.wait_ge(sqs_ready, 2 * (g + i) + 2)
                if after_first(g, i):
                    pe.wait_ge(meansq_ready, g + i + 1)
                for t in range(TILES):
                    nc.tensor.matmul(psQ[:, t:t + 1], sqs[:, 0, t * P:(t + 1) * P], ones[:, 0:1],
                                     start=True, stop=False)
                    last = nc.tensor.matmul(psQ[:, t:t + 1], sqs[:, 1, t * P:(t + 1) * P], ones[:, 0:1],
                                            start=False, stop=True)
                last.then_inc(q_done, 1)

            def project_down(s, i):
                g = s - GROUPS
                pe.wait_ge(hlo_ready, 4 * (g + i) + 4)
                pe.wait_ge(x2_ready, GROUPS)
                if after_first(g, i):
                    pe.wait_ge(x3_ready, g + i + 1)
                u = s % 2
                for t in range(TILES):
                    for c in range(FC):
                        w = tern[:, 1, c * P:(c + 1) * P]
                        nc.tensor.matmul(psO[:, t, :], h_hi[:, u, c, t * P:(t + 1) * P], w,
                                         start=(c == 0), stop=False)
                        last = nc.tensor.matmul(psO[:, t, :], h_lo[:, u, c, t * P:(t + 1) * P], w,
                                                start=False, stop=(c == FC - 1))
                last.then_inc(down_done, 1)

            def step(s, i):
                if s == 0:
                    transposes(0, 0)
                    pe.wait_ge(prep, 11)
                    project_keys(0, 0)
                    project_values(0, 0)
                if s + 1 < B_END:
                    transposes(s + 1, i)
                if s < A_END:
                    scores(s, i)
                    if s + 1 < A_END:
                        project_keys(s + 1, i)
                    if s >= 1:
                        weigh_values(s - 1, i)
                    if s + 1 < A_END:
                        project_values(s + 1, i)
                else:
                    if s == A_END:
                        weigh_values(A_END - 1, 0)
                        pe.wait_ge(prep, 13)
                    if s < B_END:
                        project_up(s, i)
                    if s > A_END:
                        sum_squares(s - 1, i)
                        project_down(s - 1, i)

            run_steps(pe, step)


def kernel(L0_attn_x, L0_attn_W, L0_attn_b, L0_ffn_w_up, L0_ffn_w_down):
    import numpy as np
    import concourse.bacc as bacc
    from concourse.bass_utils import run_bass_kernel_spmd

    x = np.ascontiguousarray(L0_attn_x)
    w = np.asarray(L0_attn_W).reshape(3, P, P)
    b = np.asarray(L0_attn_b).reshape(3, P)
    f = L0_ffn_w_up.shape[0]
    arrays = {
        "x": x,
        "w": np.ascontiguousarray(np.stack([w[0], w[1], w[2].T], axis=1)),
        "b_cols": np.ascontiguousarray(b.T),
        "b_v": np.ascontiguousarray(b[2:3]),
        "w_up_t": np.ascontiguousarray(np.asarray(L0_ffn_w_up).T),
        "w_down_t": np.ascontiguousarray(
            np.asarray(L0_ffn_w_down).T.reshape(f // P, P, P).transpose(1, 0, 2).reshape(P, f)),
    }
    nc = bacc.Bacc("TRN2", target_bir_lowering=False, num_devices=1)
    args = [nc.dram_tensor(f"in_{name}", a.shape, mybir.dt.from_np(a.dtype), kind="ExternalInput").ap()
            for name, a in arrays.items()]
    out = nc.dram_tensor("out", x.shape, F32, kind="ExternalOutput").ap()
    build(nc, *args, out)
    r = run_bass_kernel_spmd(nc, [{f"in_{name}": a for name, a in arrays.items()}], core_ids=[0])
    return r.results[0]["out"]
```

```python
from contextlib import ExitStack

import concourse.bass as bass
from concourse import mybir

P = 128
F32 = mybir.dt.float32
F16 = mybir.dt.float16
ALU = mybir.AluOpType
ACT = mybir.ActivationFunctionType
AX = mybir.AxisListType

LN_EPS = 1e-5
RMS_EPS = 1e-8

S_N = 2.0**12
S_W = 2.0**12
S_M = 2.0**8
S_P = 2.0**12
S_V = 2.0**8
S_H = 2.0**8
LN_S_P = 8.317766166719343


def build(nc, x_d, w_d, bcol_d, bv_d, wup_d, wdn_d, out_d):
    GROUPS, TOKENS, D = x_d.shape
    F = wup_d.shape[1]
    TILES = TOKENS // P
    FC = F // P
    P_SPLIT = TILES - 1
    H_SPLIT = FC - 1
    assert D == P and w_d.shape == (P, 3, D) and FC == 4 and TILES == 4 and GROUPS == 8

    x_v = x_d.rearrange("g (p t) d -> g p (t d)", t=TILES)
    out_v = out_d.rearrange("g (p t) d -> g p (t d)", t=TILES)

    with ExitStack() as ctx:
        def sb(name, shape, dt=F32):
            return ctx.enter_context(nc.sbuf_tensor(name, shape, dt))

        def psum(name, shape, dt=F32):
            return ctx.enter_context(nc.psum_tensor(name, shape, dt))

        def sem(name):
            return ctx.enter_context(nc.semaphore(name))

        x = sb("x", [P, GROUPS, TILES * D])
        w_nat = sb("w_nat", [P, 3, D])
        b_col = sb("b_col", [P, 3])
        b_v = sb("b_v", [P, D])
        bk_sel = sb("bk_sel", [P, P])
        ffn_w = sb("ffn_w", [P, 2, F])
        part = sb("part", [P, P])
        b_abs = sb("b_abs", [P, 3])
        mcol = sb("mcol", [P, 1])
        diag = sb("diag", [P, 4])
        tot = sb("tot", [P, 3])
        wsum = sb("wsum", [P, 2])
        rcp = sb("rcp", [P, 4])
        akq = sb("akq", [P, 1])
        scl = sb("scl", [P, 8])
        ident = sb("ident", [P, P])
        ones = sb("ones", [P, P])
        big = sb("big", [P, TOKENS], F16)
        m_hi = sb("m_hi", [P, P], F16)
        m_lo = sb("m_lo", [P, P], F16)
        wv_hi = sb("wv_hi", [P, P], F16)
        wv_lo = sb("wv_lo", [P, P], F16)
        c_hi = sb("c_hi", [P, P], F16)
        c_lo = sb("c_lo", [P, P], F16)
        c_mix = sb("c_mix", [P, P], F16)
        bv_hi = sb("bv_hi", [P, P], F16)
        bv_lo = sb("bv_lo", [P, P], F16)
        bv_mix = sb("bv_mix", [P, P], F16)
        t_gt = sb("t_gt", [P, 2, F], F16)
        t_lt = sb("t_lt", [P, 2, F], F16)
        tern = sb("tern", [P, 2, F], F16)
        tern32 = sb("tern32", [P, D])
        xs = sb("xs", [P, 2, TILES * D])
        bn = sb("bn", [P, 2, TILES, 6])
        mv = sb("mv", [P, 2, TILES, 2])
        nmean = sb("nmean", [P, 2, TILES])
        var2 = sb("var2", [P, 2, 2, TILES])
        root = sb("root", [P, 2, 2, TILES])
        den = sb("den", [P, 2, TILES])
        rstd = sb("rstd", [P, 2, TILES])
        p_half = sb("p_half", [P, 2, TILES])
        m_half = sb("m_half", [P, TILES])
        xn = sb("xn", [P, 2, TILES * D])
        xT_hi = sb("xT_hi", [P, 2, TOKENS], F16)
        xT_lo = sb("xT_lo", [P, 2, TOKENS], F16)
        kq_hi = sb("kq_hi", [P, TOKENS], F16)
        kq_lo = sb("kq_lo", [P, TOKENS], F16)
        nmax = sb("nmax", [P, TILES])
        nbias = sb("nbias", [P, TILES])
        prob = sb("prob", [P, P_SPLIT, TOKENS])
        prob32 = sb("prob32", [P, 2, TOKENS])
        p_hi = sb("p_hi", [P, 2, P_SPLIT, TOKENS], F16)
        p_lo = sb("p_lo", [P, 2, P_SPLIT, TOKENS], F16)
        psums = sb("psums", [P, TILES])
        rsums = sb("rsums", [P, TILES])
        v_s = sb("v_s", [P, 2, TILES, D])
        v_hi = sb("v_hi", [P, 2, P_SPLIT, D], F16)
        v_lo = sb("v_lo", [P, 2, P_SPLIT, D], F16)
        h = sb("h", [P, H_SPLIT, TOKENS])
        h32 = sb("h32", [P, 2, TOKENS])
        h_hi = sb("h_hi", [P, 2, H_SPLIT, TOKENS], F16)
        h_lo = sb("h_lo", [P, 2, H_SPLIT, TOKENS], F16)
        sq = sb("sq", [P, FC, TOKENS])
        sqs = sb("sqs", [P, 2, TOKENS])
        meansq = sb("meansq", [P, TILES])
        rms = sb("rms", [P, TILES])
        rmsd = sb("rmsd", [P, TILES])
        rrms = sb("rrms", [P, TILES])

        psT = psum("psT", [P, TOKENS])
        psV = psum("psV", [P, TILES, D])
        psS = [psum(f"psS{i}", [P, TOKENS]) for i in range(4)]
        psO = psum("psO", [P, TILES, D])
        psQ = psum("psQ", [P, TOKENS])
        psW = psQ

        w_loaded = sem("w_loaded")
        bcol_loaded = sem("bcol_loaded")
        bv_loaded = sem("bv_loaded")
        up_loaded = sem("up_loaded")
        dn_loaded = sem("dn_loaded")
        x_loaded = sem("x_loaded")
        xs_loaded = [sem("xs_loaded_even"), sem("xs_loaded_odd")]
        consts_ready = sem("consts_ready")
        ident_ready = sem("ident_ready")
        prep = sem("prep")
        pe_prep = sem("pe_prep")
        act_prep = sem("act_prep")
        rcp_ready = sem("rcp_ready")
        wsum_ready = sem("wsum_ready")
        wsum_total = sem("wsum_total")
        tern_step = sem("tern_step")
        bn_done = sem("bn_done")
        stats_ready = sem("stats_ready")
        pool_a = sem("pool_a")
        pool_b = sem("pool_b")
        rstd_done = sem("rstd_done")
        norm_stats = sem("norm_stats")
        root_ready = sem("root_ready")
        den_ready = sem("den_ready")
        rstd_ready = sem("rstd_ready")
        xn_ready = sem("xn_ready")
        xn_dve = sem("xn_dve")
        t_done = sem("t_done")
        xhi_ready = sem("xhi_ready")
        xlo_ready = sem("xlo_ready")
        k_done = sem("k_done")
        kqhi_ready = sem("kqhi_ready")
        kqlo_ready = sem("kqlo_ready")
        v_done = sem("v_done")
        scores_done = sem("scores_done")
        max_done = sem("max_done")
        bias_ready = sem("bias_ready")
        exp_done = sem("exp_done")
        phi_ready = sem("phi_ready")
        plo_ready = sem("plo_ready")
        rsum_ready = sem("rsum_ready")
        vs_ready = sem("vs_ready")
        vhi_ready = sem("vhi_ready")
        vlo_ready = sem("vlo_ready")
        pv_done = sem("pv_done")
        x2_ready = sem("x2_ready")
        up_done = sem("up_done")
        gelu_done = sem("gelu_done")
        hhi_act = sem("hhi_act")
        hhi_dve = sem("hhi_dve")
        hlo_ready = sem("hlo_ready")
        sq_ready = sem("sq_ready")
        sqs_ready = sem("sqs_ready")
        q_done = sem("q_done")
        meansq_ready = sem("meansq_ready")
        rms_ready = sem("rms_ready")
        rrms_ready = sem("rrms_ready")
        down_done = sem("down_done")
        x3_ready = sem("x3_ready")
        stored = sem("stored")
        pool_gate = sem("pool_gate")
        dve_gate = sem("dve_gate")
        sp_gate = sem("sp_gate")

        EXP_SCALE, OUT_SCALE, M_SCALE, V_SCALE, T_UP, T_DN, NT_UP, NT_DN = range(8)

        A_END, B_END = GROUPS, 2 * GROUPS
        LOOPS = ((2, 6), (GROUPS + 1, GROUPS + 5))

        def after_first(g, i):
            return g >= 1 or not isinstance(i, int)

        def run_steps(eng, step):
            s = 0
            while s <= B_END:
                loop = [b for a, b in LOOPS if a == s]
                if loop:
                    with eng.Fori(0, loop[0] - s - 1, 2) as i:
                        step(s, i)
                        step(s + 1, i)
                    s = loop[0]
                else:
                    step(s, 0)
                    s += 1

        FFN_POOL = "Wnr01"
        FFN_DVE = "s0hnlcq1i2ra"
        HI_ON_ACT = (0, 2)

        POOL_TILES = 3

        def h_chunk(s, c):
            return h[:, c, :] if c < H_SPLIT else h32[:, s % 2, :]

        block = ctx.enter_context(nc.Block())

        @block.sync
        def _(sp):
            sp.dma_start(xs[:, 0, :], x_v[0]).then_inc(xs_loaded[0], 16)
            sp.dma_start(w_nat[:, :, :], w_d).then_inc(w_loaded, 16)
            sp.dma_start(xs[:, 1, :], x_v[1]).then_inc(xs_loaded[1], 16)
            sp.wait_ge(dn_loaded, 16)
            sp.wait_ge(xs_loaded[1], 16)
            sp.dma_start(x[:, :, :], x_d.rearrange("g (p t) d -> p g (t d)", t=TILES)).then_inc(x_loaded, 16)
            with sp.Fori(2, GROUPS - 1, 2) as i:
                for u in range(2):
                    sp.wait_ge(xn_ready, i + u - 1)
                    sp.sem_inc(sp_gate, 1)
                    sp.dma_start(xs[:, u, :], x_v[bass.ds(i + u, 1)].rearrange("g p n -> p (g n)")
                                 ).then_inc(xs_loaded[u], 16)
            with sp.Fori(0, GROUPS - 1, 2) as i:
                for u in range(2):
                    sp.wait_ge(xn_ready, i + u + GROUPS - 1)
                    sp.sem_inc(sp_gate, 1)
                    sp.wait_ge(xn_dve, i + u + 1)
                    sp.sem_inc(sp_gate, 1)
                    sp.wait_ge(x2_ready, i + u + 1)
                    sp.sem_inc(sp_gate, 1)
                    sp.dma_start(xs[:, u, :], x[:, bass.ds(i + u, 1), :].rearrange("p g n -> p (g n)")
                                 ).then_inc(xs_loaded[u], 16)
            with sp.Fori(0, GROUPS, 1) as i:
                sp.wait_ge(x3_ready, i + 2)
                sp.dma_start(out_v[bass.ds(i, 1)].rearrange("g p n -> p g n"),
                             x[:, bass.ds(i, 1), :]).then_inc(stored, 16)
            sp.wait_ge(stored, 16 * GROUPS)

        @block.scalar
        def _(act):
            act.dma_start(b_col[:, :], bcol_d).then_inc(bcol_loaded, 16)
            act.wait_ge(consts_ready, 1)
            for row in (0, 64):
                act.dma_start(b_v[row:row + 1, :], bv_d).then_inc(bv_loaded, 16)
            act.dma_start(ffn_w[:, 0, :], wup_d).then_inc(up_loaded, 16)
            act.dma_start(ffn_w[:, 1, :], wdn_d).then_inc(dn_loaded, 16)

            act.wait_ge(prep, 8)
            nc.scalar.activation(m_hi[:, :], psS[0][:, 0:P], ACT.Identity,
                                 scale=scl[:, M_SCALE:M_SCALE + 1])
            nc.scalar.activation(c_hi[:, :], psS[0][:, P:2 * P], ACT.Identity,
                                 scale=scl[:, M_SCALE:M_SCALE + 1]).then_inc(act_prep, 1)

            def value_heads():
                act.wait_ge(bv_loaded, 32)
                nc.scalar.activation(bv_hi[:, :], b_v[:, :], ACT.Identity,
                                     scale=scl[:, V_SCALE:V_SCALE + 1])
                nc.scalar.activation(wv_hi[:, :], w_nat[:, 2, :], ACT.Identity,
                                     scale=scl[:, V_SCALE:V_SCALE + 1]).then_inc(act_prep, 1)

            def weight_sums():
                act.wait_ge(up_loaded, 16)
                nc.scalar.activation(sq[:, 0, :], ffn_w[:, 0, :], ACT.Abs, accum_out=wsum[:, 0:1])
                act.wait_ge(dn_loaded, 16)
                nc.scalar.activation(sq[:, 1, :], ffn_w[:, 1, :], ACT.Abs, accum_out=wsum[:, 1:2]).then_inc(wsum_ready, 1)

            def x_head(n, i):
                act.wait_ge(t_done, n + 1 + i)
                nc.scalar.copy(xT_hi[:, n % 2, :], psT[:, :]).then_inc(xhi_ready, 1)

            def kq_head(n, i):
                act.wait_ge(k_done, n + 1 + i)
                nc.scalar.mul(kq_hi[:, :], psT[:, :], 1.0 / (S_N * S_M)).then_inc(kqhi_ready, 1)

            def exp(s, i, j):
                act.wait_ge(bias_ready, 2 * (s + i) + j // 2 + 1)
                if s >= 1 and j < P_SPLIT:
                    act.wait_ge(plo_ready, P_SPLIT * (s - 1 + i) + j + 1)
                    if j == 0:
                        act.wait_ge(rsum_ready, s + i)
                out = prob[:, j, :] if j < P_SPLIT else prob32[:, s % 2, :]
                nc.scalar.activation(out, psS[j][:, :], ACT.Exp, bias=nbias[:, j:j + 1],
                                     scale=scl[:, EXP_SCALE:EXP_SCALE + 1],
                                     accum_out=psums[:, j:j + 1]).then_inc(exp_done, 1)

            def p_head(s, i, j):
                act.wait_ge(exp_done, 4 * (s + i) + j + 1)
                nc.scalar.copy(p_hi[:, s % 2, j, :], prob[:, j, :]).then_inc(phi_ready, 1)

            def v_head(s, i):
                act.wait_ge(vs_ready, s + 1 + i)
                nc.scalar.copy(v_hi[:, s % 2, :, :], v_s[:, s % 2, 0:P_SPLIT, :]).then_inc(vhi_ready, 1)

            def gelu(s, i, c):
                g = s - GROUPS
                act.wait_ge(up_done, 4 * (g + i) + c + 1)
                if g >= 1 and c < H_SPLIT:
                    act.wait_ge(hlo_ready, H_SPLIT * (g - 1 + i) + c + 1)
                nc.scalar.activation(h_chunk(s, c), psS[c][:, :], ACT.Gelu, scale=1.0 / S_N).then_inc(gelu_done, 1)

            def h_head_and_square(s, i, c):
                g = s - GROUPS
                act.wait_ge(gelu_done, 4 * (g + i) + c + 1)
                if c in HI_ON_ACT:
                    nc.scalar.mul(h_hi[:, s % 2, c, :], h[:, c, :], S_H).then_inc(hhi_act, 1)
                if g >= 1 and c % 2 == 0:
                    act.wait_ge(sqs_ready, 2 * (g - 1 + i) + c // 2 + 1)
                nc.scalar.square(sq[:, c, :], h_chunk(s, c)).then_inc(sq_ready, 1)

            def step(s, i):
                if s == 0:
                    x_head(0, 0)
                    value_heads()
                    weight_sums()
                    kq_head(0, 0)
                if s + 1 < B_END:
                    x_head(s + 1, i)
                if 1 <= s <= A_END:
                    v_head(s - 1, i)
                    p_head(s - 1, i, 1)
                    p_head(s - 1, i, 2)
                if s < A_END:
                    exp(s, i, 0)
                    exp(s, i, 1)
                    if s + 1 < A_END:
                        kq_head(s + 1, i)
                    p_head(s, i, 0)
                    exp(s, i, 2)
                    exp(s, i, 3)
                elif s < B_END:
                    gelu(s, i, 0)
                    for c in range(1, FC):
                        gelu(s, i, c)
                        h_head_and_square(s, i, c - 1)
                    h_head_and_square(s, i, FC - 1)

            run_steps(act, step)

        @block.gpsimd
        def _(pool):
            nc.gpsimd.memset(b_v[:, :], 0.0).then_inc(consts_ready, 1)
            nc.gpsimd.memset(p_half[:, :, :], 0.5)
            nc.gpsimd.memset(m_half[:, :], -0.5).then_inc(pool_b, 1)
            nc.gpsimd.memset(ident[:, :], 0.0).then_inc(pool_a, 1)
            pool.wait_ge(pool_a, 1)
            nc.gpsimd.affine_select(out=ident[:, :], in_=ident[:, :], compare_op=ALU.not_equal, fill=1.0,
                                    base=0, pattern=[[-1, P]], channel_multiplier=1).then_inc(ident_ready, 1)
            pool.wait_ge(pool_b, 1)

            def roots(n, i):
                u = n % 2
                pool.wait_ge(norm_stats, n + 1 + i)
                if n < GROUPS:
                    nc.gpsimd.tensor_tensor(rstd[:, u, :], var2[:, u, 1, :], m_half[:, :],
                                            ALU.pow).then_inc(rstd_done, 1)
                else:
                    nc.gpsimd.tensor_tensor(root[:, u, :, :], var2[:, u, :, :], p_half[:, :, :],
                                            ALU.pow).then_inc(root_ready, 1)

            def apply_norm(n, i):
                u = n % 2
                if n >= 2:
                    pool.wait_ge(t_done, n - 1 + i)
                if n >= GROUPS:
                    pool.wait_ge(rstd_ready, n - GROUPS + 1 + i)
                else:
                    pool.wait_ge(rstd_done, n + 1 + i)
                pool.sem_inc(pool_gate, 1)
                for t in range(TILES if n < GROUPS else POOL_TILES):
                    last = nc.gpsimd.tensor_scalar(xn[:, u, t * D:(t + 1) * D], xs[:, u, t * D:(t + 1) * D],
                                                   nmean[:, u, t:t + 1], rstd[:, u, t:t + 1], ALU.add, ALU.mult)
                last.then_inc(xn_ready, 1)

            def p_rest(s, i, j):
                pool.wait_ge(phi_ready, P_SPLIT * (s + i) + j + 1)
                nc.gpsimd.tensor_tensor(p_lo[:, s % 2, j, :], prob[:, j, :], p_hi[:, s % 2, j, :],
                                        ALU.subtract).then_inc(plo_ready, 1)

            def add_squares(s, i, k):
                g = s - GROUPS
                pool.wait_ge(sq_ready, 4 * (g + i) + 2 * k + 2)
                if g >= 1 and k == 0:
                    pool.wait_ge(q_done, g + i)
                nc.gpsimd.tensor_tensor(sqs[:, k, :], sq[:, 2 * k, :], sq[:, 2 * k + 1, :],
                                        ALU.add).then_inc(sqs_ready, 1)

            def root_meansq(s, i):
                g = s - GROUPS
                pool.wait_ge(meansq_ready, g + 2 + i)
                nc.gpsimd.tensor_tensor(rms[:, :], meansq[:, :], p_half[:, 0, :], ALU.pow).then_inc(rms_ready, 1)

            def step(s, i):
                if s == 0:
                    roots(0, 0)
                    roots(1, 0)
                if s < A_END:
                    roots(s + 2, i)
                if 1 <= s <= A_END:
                    p_rest(s - 1, i, 1)
                    p_rest(s - 1, i, 2)
                if s < A_END:
                    apply_norm(s + 2, i)
                    p_rest(s, i, 0)
                    if s == A_END - 1 and "R" in FFN_POOL:
                        roots(s + 3, 0)
                elif s < B_END:
                    for what in FFN_POOL:
                        if what == "r" and s > A_END:
                            root_meansq(s - 1, i)
                        if what == "W" and s + 2 < B_END:
                            roots(s + 2, i)
                        if what == "R" and s + 3 < B_END:
                            roots(s + 3, i)
                        if what == "n" and s + 2 < B_END:
                            apply_norm(s + 2, i)
                        if what in "01":
                            add_squares(s, i, int(what))
                else:
                    root_meansq(s - 1, i)

            run_steps(pool, step)

        @block.vector
        def _(dve):
            def x_at(n, i):
                slot = n % GROUPS
                if isinstance(i, int):
                    return x[:, slot + i, :]
                return x[:, bass.ds(slot + i, 1), :].rearrange("p a n -> p (a n)")

            def token_stats(n, i):
                u = n % 2
                dve.wait_ge(xs_loaded[u], 16 * (n // 2) + 16 + 8 * i)
                for t in range(TILES):
                    last = nc.vector.bn_stats(bn[:, u, t, :], xs[:, u, t * D:(t + 1) * D])
                last.then_inc(bn_done, 1)

            def combine_stats(n, i):
                u = n % 2
                if n >= 2:
                    dve.wait_ge(xn_ready, n - 1 + i)
                dve.wait_ge(bn_done, n + 1 + i)
                dve.sem_inc(dve_gate, 1)
                for t in range(TILES):
                    last = nc.vector.bn_aggr(mv[:, u, t, :], bn[:, u, t, :])
                last.then_inc(stats_ready, 1)

            def norm_inputs(n, i):
                u = n % 2
                dve.wait_ge(stats_ready, n + 1 + i)
                var = mv[:, u, :, 1]
                nc.vector.tensor_scalar(nmean[:, u, :], mv[:, u, :, 0], -1.0, None, ALU.mult)
                nc.vector.tensor_scalar(var2[:, u, 0, :], var, S_N**-2, None, ALU.mult)
                nc.vector.tensor_scalar(var2[:, u, 1, :], var, LN_EPS, S_N**-2, ALU.add,
                                        ALU.mult).then_inc(norm_stats, 1)

            def apply_first(n):
                dve.wait_ge(rstd_done, n + 1)
                for t in range(TILES):
                    last = nc.vector.tensor_scalar(xn[:, n, t * D:(t + 1) * D], xs[:, n, t * D:(t + 1) * D],
                                                   nmean[:, n, t:t + 1], rstd[:, n, t:t + 1], ALU.add, ALU.mult)
                last.then_inc(xn_ready, 1)

            def x_rest(n, i):
                dve.wait_ge(xhi_ready, n + 1 + i)
                nc.vector.scalar_tensor_tensor(out=xT_lo[:, n % 2, :], in0=psT[:, :], scalar=1.0,
                                               in1=xT_hi[:, n % 2, :], op0=ALU.mult,
                                               op1=ALU.subtract).then_inc(xlo_ready, 1)

            dve.sem_inc(xn_dve, 2)
            dve.sem_inc(meansq_ready, 1)
            dve.sem_inc(rms_ready, 1)
            dve.sem_inc(x3_ready, 1)
            nc.vector.memset(part[:, :], 0.0)
            nc.vector.memset(bk_sel[:, :], 0.0)
            nc.vector.memset(ones[:, :], 1.0)
            nc.vector.memset(c_mix[:, :], 0.0)
            nc.vector.memset(bv_mix[:, :], 0.0).then_inc(prep, 1)
            nc.vector.memset(big[:, :], S_N)
            token_stats(0, 0)
            dve.wait_ge(prep, 1)
            dve.wait_ge(bcol_loaded, 16)
            nc.vector.tensor_scalar(b_abs[:, :], b_col[:, :], -1.0, None, ALU.mult)
            nc.vector.tensor_copy(bk_sel[:, 0:1], b_col[:, 1:2])
            nc.vector.tensor_copy(bk_sel[:, 64:65], b_col[:, 1:2]).then_inc(prep, 1)
            combine_stats(0, 0)
            dve.wait_ge(prep, 2)
            nc.vector.tensor_tensor(b_abs[:, :], b_abs[:, :], b_col[:, :], ALU.max)
            dve.wait_ge(w_loaded, 16)
            nc.vector.tensor_reduce(part[:, 0:3], w_nat[:, :, :], AX.X, ALU.max,
                                    apply_absolute_value=True).then_inc(prep, 1)
            norm_inputs(0, 0)
            dve.wait_ge(prep, 3)
            nc.vector.tensor_tensor(part[:, 0:3], part[:, 0:3], b_abs[:, :], ALU.max).then_inc(prep, 1)
            token_stats(1, 0)
            dve.wait_ge(pe_prep, 1)
            nc.vector.reduce_max(mcol[:, :], psW[:, 0:P], AX.X).then_inc(prep, 1)
            combine_stats(1, 0)
            dve.wait_ge(prep, 5)
            nc.vector.tensor_scalar(diag[:, 0:3], ident[:, 0:3], mcol[:, 0:1], None, ALU.mult).then_inc(prep, 1)
            norm_inputs(1, 0)
            apply_first(0)
            dve.wait_ge(pe_prep, 2)
            nc.vector.tensor_scalar(tot[:, 0:3], psW[:, P:P + 3], 1e-30, None, ALU.max).then_inc(prep, 1)
            dve.wait_ge(prep, 7)
            nc.vector.reciprocal(rcp[:, 0:3], tot[:, 0:3]).then_inc(rcp_ready, 1)
            nc.vector.tensor_scalar(scl[:, EXP_SCALE:EXP_SCALE + 1], tot[:, 0:1], tot[:, 1:2],
                                    1.0 / (D * S_N), ALU.mult, ALU.mult)
            nc.vector.tensor_scalar(scl[:, OUT_SCALE:OUT_SCALE + 1], tot[:, 2:3], 1.0 / (S_P * S_V), None,
                                    ALU.mult)
            dve.wait_ge(rcp_ready, 1)
            nc.vector.tensor_scalar(scl[:, M_SCALE:M_SCALE + 1], rcp[:, 0:1], rcp[:, 1:2], S_M, ALU.mult, ALU.mult)
            nc.vector.tensor_scalar(scl[:, V_SCALE:V_SCALE + 1], rcp[:, 2:3], S_W, None,
                                    ALU.mult).then_inc(prep, 1)
            dve.wait_ge(prep, 8)
            dve.wait_ge(act_prep, 1)
            nc.vector.scalar_tensor_tensor(out=m_lo[:, :], in0=psS[0][:, 0:P], scalar=scl[:, M_SCALE:M_SCALE + 1],
                                           in1=m_hi[:, :], op0=ALU.mult, op1=ALU.subtract)
            nc.vector.scalar_tensor_tensor(out=c_mix[64:65, :], in0=psS[0][64:65, P:2 * P],
                                           scalar=scl[64:65, M_SCALE:M_SCALE + 1],
                                           in1=c_hi[64:65, :], op0=ALU.mult, op1=ALU.subtract)
            nc.vector.tensor_copy(c_mix[0:1, :], c_hi[0:1, :]).then_inc(prep, 1)
            x_rest(0, 0)
            apply_first(1)
            dve.wait_ge(act_prep, 2)
            nc.vector.scalar_tensor_tensor(out=bv_mix[64:65, :], in0=b_v[64:65, :],
                                           scalar=scl[64:65, V_SCALE:V_SCALE + 1],
                                           in1=bv_hi[64:65, :], op0=ALU.mult, op1=ALU.subtract)
            nc.vector.tensor_copy(bv_mix[0:1, :], bv_hi[0:1, :])
            nc.vector.scalar_tensor_tensor(out=wv_lo[:, :], in0=w_nat[:, 2, :],
                                           scalar=scl[:, V_SCALE:V_SCALE + 1],
                                           in1=wv_hi[:, :], op0=ALU.mult, op1=ALU.subtract).then_inc(prep, 1)

            def ternary_weights():
                dve.wait_ge(wsum_total, 1)
                nc.vector.tensor_scalar(scl[:, T_UP:T_DN + 1], psQ[:, 0:2], 0.5 / (F * D), None, ALU.mult)
                nc.vector.tensor_scalar(scl[:, NT_UP:NT_DN + 1], psQ[:, 0:2], -0.5 / (F * D), None,
                                        ALU.mult).then_inc(tern_step, 1)
                dve.wait_ge(tern_step, 1)
                for k in range(2):
                    src = ffn_w[:, k, :]
                    nc.vector.tensor_scalar(t_gt[:, k, :], src, scl[:, T_UP + k:T_UP + k + 1], None, ALU.is_gt)
                    last = nc.vector.tensor_scalar(t_lt[:, k, :], src, scl[:, NT_UP + k:NT_UP + k + 1], None,
                                                   ALU.is_lt)
                last.then_inc(tern_step, 1)
                dve.wait_ge(tern_step, 2)
                nc.vector.tensor_tensor(tern[:, :, :], t_gt[:, :, :], t_lt[:, :, :],
                                        ALU.subtract).then_inc(tern_step, 1)
                dve.wait_ge(tern_step, 3)
                nc.vector.tensor_scalar(tern32[:, :], tern[:, 1, H_SPLIT * D:FC * D], S_H, None,
                                        ALU.mult).then_inc(tern_step, 1)

            def kq_rest(n, i):
                dve.wait_ge(kqhi_ready, n + 1 + i)
                nc.vector.scalar_tensor_tensor(out=kq_lo[:, :], in0=psT[:, :], scalar=1.0 / (S_N * S_M),
                                               in1=kq_hi[:, :], op0=ALU.mult,
                                               op1=ALU.subtract).then_inc(kqlo_ready, 1)

            def maximum(s, i, j):
                n = 4 * (s + i) + j + 1
                dve.wait_ge(scores_done, n)
                nc.vector.tensor_reduce(nmax[:, j:j + 1], psS[j][:, :], AX.X, ALU.max,
                                        negate=True).then_inc(max_done, 1)

            def exp_bias(s, i, k):
                dve.wait_ge(max_done, 4 * (s + i) + 2 * k + 2)
                nc.vector.tensor_scalar(nbias[:, 2 * k:2 * k + 2], nmax[:, 2 * k:2 * k + 2], scl[:, EXP_SCALE:EXP_SCALE + 1],
                                        LN_S_P, ALU.mult, ALU.add).then_inc(bias_ready, 1)

            def divide_values(s, i):
                dve.wait_ge(exp_done, 4 * (s + i) + 4)
                nc.vector.reciprocal(rsums[:, :], psums[:, :]).then_inc(rsum_ready, 1)
                dve.wait_ge(rsum_ready, s + 1 + i)
                dve.wait_ge(v_done, s + 1 + i)
                nc.vector.scalar_tensor_tensor(
                    out=v_s[:, s % 2, :, :], in0=psV[:, :, :], scalar=S_V * S_P / (S_N * S_W),
                    in1=rsums[:, :].unsqueeze(2).to_broadcast([P, TILES, D]),
                    op0=ALU.mult, op1=ALU.mult).then_inc(vs_ready, 1)

            def v_rest(s, i):
                dve.wait_ge(vhi_ready, s + 1 + i)
                nc.vector.tensor_tensor(v_lo[:, s % 2, :, :], v_s[:, s % 2, 0:P_SPLIT, :], v_hi[:, s % 2, :, :],
                                        ALU.subtract).then_inc(vlo_ready, 1)

            def add_attention(s, i):
                if s == 0:
                    dve.wait_ge(x_loaded, 16)
                dve.wait_ge(pv_done, s + 1 + i)
                xg = x_at(s, i)
                nc.vector.scalar_tensor_tensor(out=xg, in0=psO[:, :, :].rearrange("p t d -> p (t d)"),
                                               scalar=scl[:, OUT_SCALE:OUT_SCALE + 1], in1=xg,
                                               op0=ALU.mult, op1=ALU.add).then_inc(x2_ready, 1)

            def norm_reciprocal(n, i):
                u = n % 2
                dve.wait_ge(root_ready, n - GROUPS + 1 + i)
                nc.vector.scalar_tensor_tensor(out=den[:, u, :], in0=root[:, u, 1, :], scalar=RMS_EPS,
                                               in1=root[:, u, 0, :], op0=ALU.mult,
                                               op1=ALU.add).then_inc(den_ready, 1)
                dve.wait_ge(den_ready, n - GROUPS + 1 + i)
                nc.vector.reciprocal(rstd[:, u, :], den[:, u, :]).then_inc(rstd_ready, 1)

            def apply_last(n, i):
                u = n % 2
                t = TILES - 1
                dve.wait_ge(rstd_ready, n - GROUPS + 1 + i)
                dve.wait_ge(t_done, n - 1 + i)
                nc.vector.tensor_scalar(xn[:, u, t * D:(t + 1) * D], xs[:, u, t * D:(t + 1) * D],
                                        nmean[:, u, t:t + 1], rstd[:, u, t:t + 1], ALU.add,
                                        ALU.mult).then_inc(xn_dve, 1)

            def h_head(s, i, c):
                g = s - GROUPS
                dve.wait_ge(gelu_done, 4 * (g + i) + c + 1)
                nc.vector.tensor_scalar(h_hi[:, s % 2, c, :], h[:, c, :], S_H, None, ALU.mult).then_inc(hhi_dve, 1)

            def h_rest(s, i, c):
                g = s - GROUPS
                if c in HI_ON_ACT:
                    dve.wait_ge(hhi_act, len(HI_ON_ACT) * (g + i) + HI_ON_ACT.index(c) + 1)
                else:
                    dve.wait_ge(hhi_dve, (H_SPLIT - len(HI_ON_ACT)) * (g + i) + c // 2 + 1)
                nc.vector.scalar_tensor_tensor(out=h_lo[:, s % 2, c, :], in0=h[:, c, :], scalar=S_H,
                                               in1=h_hi[:, s % 2, c, :], op0=ALU.mult,
                                               op1=ALU.subtract).then_inc(hlo_ready, 1)

            def mean_square(s, i):
                g = s - GROUPS
                dve.wait_ge(q_done, g + 1 + i)
                if after_first(g, i):
                    dve.wait_ge(rms_ready, g + i + 1)
                nc.vector.tensor_scalar(meansq[:, :], psQ[:, 0:TILES], 1.0 / F, None, ALU.mult).then_inc(meansq_ready, 1)

            def rms_reciprocal(s, i):
                g = s - GROUPS
                dve.wait_ge(rms_ready, g + 2 + i)
                nc.vector.tensor_scalar(rmsd[:, :], rms[:, :], RMS_EPS, S_H, ALU.add, ALU.mult).then_inc(rrms_ready, 1)
                dve.wait_ge(rrms_ready, 2 * (g + i) + 1)
                nc.vector.reciprocal(rrms[:, :], rmsd[:, :]).then_inc(rrms_ready, 1)

            def add_ffn(s, i):
                g = s - GROUPS
                dve.wait_ge(rrms_ready, 2 * (g + i) + 2)
                dve.wait_ge(down_done, g + 1 + i)
                xg = x_at(s, i)
                for t in range(TILES):
                    last = nc.vector.scalar_tensor_tensor(
                        out=xg[:, t * D:(t + 1) * D], in0=psO[:, t, :], scalar=rrms[:, t:t + 1],
                        in1=xg[:, t * D:(t + 1) * D], op0=ALU.mult, op1=ALU.add)
                last.then_inc(x3_ready, 1)

            def step(s, i):
                if s == 0:
                    kq_rest(0, 0)
                    token_stats(2, 0)
                    combine_stats(2, 0)
                    norm_inputs(2, 0)
                if s + 1 < B_END:
                    x_rest(s + 1, i)
                if s < A_END:
                    if s >= 1:
                        v_rest(s - 1, i)
                    maximum(s, i, 0)
                    maximum(s, i, 1)
                    exp_bias(s, i, 0)
                    if s >= 2:
                        add_attention(s - 2, i)
                    maximum(s, i, 2)
                    if s + 2 >= GROUPS:
                        norm_reciprocal(s + 2, i)
                        apply_last(s + 2, i)
                    maximum(s, i, 3)
                    exp_bias(s, i, 1)
                    if s + 1 < A_END:
                        kq_rest(s + 1, i)
                    token_stats(s + 3, i)
                    combine_stats(s + 3, i)
                    norm_inputs(s + 3, i)
                    divide_values(s, i)
                    if s == 0:
                        ternary_weights()
                elif s < B_END:
                    if s == A_END:
                        v_rest(A_END - 1, 0)
                        add_attention(A_END - 2, 0)
                    for what in FFN_DVE:
                        if what == "n" and s + 2 < B_END:
                            norm_reciprocal(s + 2, i)
                        if what == "l" and s + 2 < B_END:
                            apply_last(s + 2, i)
                        if what == "s" and s + 3 < B_END:
                            token_stats(s + 3, i)
                        if what == "c" and s + 3 < B_END:
                            combine_stats(s + 3, i)
                        if what == "i" and s + 3 < B_END:
                            norm_inputs(s + 3, i)
                        if what == "q" and s > A_END:
                            mean_square(s - 1, i)
                        if what == "r" and s > A_END:
                            rms_reciprocal(s - 1, i)
                        if what == "a" and s > A_END:
                            add_ffn(s - 1, i)
                        if what == "h":
                            h_head(s, i, 1)
                        if what in "012":
                            h_rest(s, i, int(what))
                    if s == A_END:
                        add_attention(A_END - 1, 0)
                else:
                    mean_square(s - 1, i)
                    rms_reciprocal(s - 1, i)
                    add_ffn(s - 1, i)

            run_steps(dve, step)

        @block.tensor
        def _(pe):
            pe.wait_ge(prep, 4)
            pe.wait_ge(ident_ready, 1)
            nc.tensor.transpose(psW[:, 0:P], part[:, :], ident[:, :]).then_inc(pe_prep, 1)
            nc.tensor.matmul(psS[0][:, 0:P], w_nat[:, 1, :], w_nat[:, 0, :], start=True, stop=True)
            nc.tensor.matmul(psS[0][:, P:2 * P], bk_sel[:, :], w_nat[:, 0, :], start=True, stop=True)
            pe.wait_ge(prep, 6)
            nc.tensor.matmul(psW[:, P:P + 3], ones[:, :], diag[:, 0:3], start=True, stop=True).then_inc(pe_prep, 1)

            def transposes(n, i):
                pe.wait_ge(xn_ready, n + 1 + i)
                if n >= GROUPS:
                    pe.wait_ge(xn_dve, n - GROUPS + 3 + i)
                if n >= 1:
                    pe.wait_ge(xlo_ready, n + i)
                    if n <= GROUPS:
                        pe.wait_ge(kqlo_ready, n + i)
                for t in range(TILES):
                    last = nc.tensor.transpose(psT[:, t * P:(t + 1) * P], xn[:, n % 2, t * D:(t + 1) * D],
                                               ident[:, :])
                last.then_inc(t_done, 1)

            def project_keys(n, i):
                pe.wait_ge(xlo_ready, n + 1 + i)
                nc.tensor.matmul(psT[:, :], m_hi[:, :], xT_hi[:, n % 2, :], start=True, stop=False)
                nc.tensor.matmul(psT[:, :], m_hi[:, :], xT_lo[:, n % 2, :], start=False, stop=False)
                nc.tensor.matmul(psT[:, :], m_lo[:, :], xT_hi[:, n % 2, :], start=False, stop=False)
                nc.tensor.matmul(psT[:, :], c_mix[:, :], big[:, :], start=False, stop=True).then_inc(k_done, 1)

            def project_values(n, i):
                if n >= 1:
                    pe.wait_ge(vs_ready, n + i)
                for t in range(TILES):
                    hi = xT_hi[:, n % 2, t * P:(t + 1) * P]
                    lo = xT_lo[:, n % 2, t * P:(t + 1) * P]
                    nc.tensor.matmul(psV[:, t, :], hi, wv_hi[:, :], start=True, stop=False)
                    nc.tensor.matmul(psV[:, t, :], hi, wv_lo[:, :], start=False, stop=False)
                    nc.tensor.matmul(psV[:, t, :], lo, wv_hi[:, :], start=False, stop=False)
                    last = nc.tensor.matmul(psV[:, t, :], big[:, 0:P], bv_mix[:, :], start=False, stop=True)
                last.then_inc(v_done, 1)

            def scores(s, i):
                pe.wait_ge(kqlo_ready, s + 1 + i)
                for j in range(TILES):
                    if s >= 1:
                        pe.wait_ge(exp_done, 4 * (s - 1 + i) + j + 1)
                    hi = kq_hi[:, j * P:(j + 1) * P]
                    lo = kq_lo[:, j * P:(j + 1) * P]
                    nc.tensor.matmul(psS[j][:, :], hi, xT_hi[:, s % 2, :], start=True, stop=False)
                    nc.tensor.matmul(psS[j][:, :], hi, xT_lo[:, s % 2, :], start=False, stop=False)
                    nc.tensor.matmul(psS[j][:, :], lo, xT_hi[:, s % 2, :], start=False,
                                     stop=True).then_inc(scores_done, 1)

            def weigh_values(s, i):
                pe.wait_ge(vlo_ready, s + 1 + i)
                pe.wait_ge(plo_ready, P_SPLIT * (s + i + 1))
                pe.wait_ge(exp_done, TILES * (s + i + 1))
                if after_first(s, i):
                    pe.wait_ge(x2_ready, s + i)
                u = s % 2
                for t in range(TILES):
                    for j in range(P_SPLIT):
                        hi = p_hi[:, u, j, t * P:(t + 1) * P]
                        lo = p_lo[:, u, j, t * P:(t + 1) * P]
                        nc.tensor.matmul(psO[:, t, :], hi, v_hi[:, u, j, :], start=(j == 0), stop=False)
                        nc.tensor.matmul(psO[:, t, :], hi, v_lo[:, u, j, :], start=False, stop=False)
                        nc.tensor.matmul(psO[:, t, :], lo, v_hi[:, u, j, :], start=False, stop=False)
                    last = nc.tensor.matmul(psO[:, t, :], prob32[:, u, t * P:(t + 1) * P], v_s[:, u, P_SPLIT, :],
                                            start=False, stop=True)
                last.then_inc(pv_done, 1)

            def project_up(s, i):
                g = s - GROUPS
                pe.wait_ge(xlo_ready, s + 1 + i)
                for c in range(FC):
                    if g >= 1:
                        pe.wait_ge(gelu_done, 4 * (g - 1 + i) + c + 1)
                    else:
                        pe.wait_ge(exp_done, 4 * (A_END - 1) + c + 1)
                    w = tern[:, 0, c * P:(c + 1) * P]
                    nc.tensor.matmul(psS[c][:, :], w, xT_hi[:, s % 2, :], start=True, stop=False)
                    nc.tensor.matmul(psS[c][:, :], w, xT_lo[:, s % 2, :], start=False,
                                     stop=True).then_inc(up_done, 1)

            def sum_squares(s, i):
                g = s - GROUPS
                pe.wait_ge(sqs_ready, 2 * (g + i) + 2)
                if after_first(g, i):
                    pe.wait_ge(meansq_ready, g + i + 1)
                for t in range(TILES):
                    nc.tensor.matmul(psQ[:, t:t + 1], sqs[:, 0, t * P:(t + 1) * P], ones[:, 0:1],
                                     start=True, stop=False)
                    last = nc.tensor.matmul(psQ[:, t:t + 1], sqs[:, 1, t * P:(t + 1) * P], ones[:, 0:1],
                                            start=False, stop=True)
                last.then_inc(q_done, 1)

            def project_down(s, i):
                g = s - GROUPS
                pe.wait_ge(hlo_ready, H_SPLIT * (g + i + 1))
                pe.wait_ge(gelu_done, FC * (g + i + 1))
                pe.wait_ge(x2_ready, GROUPS)
                if after_first(g, i):
                    pe.wait_ge(x3_ready, g + i + 1)
                u = s % 2
                for t in range(TILES):
                    for c in range(H_SPLIT):
                        w = tern[:, 1, c * P:(c + 1) * P]
                        nc.tensor.matmul(psO[:, t, :], h_hi[:, u, c, t * P:(t + 1) * P], w,
                                         start=(c == 0), stop=False)
                        nc.tensor.matmul(psO[:, t, :], h_lo[:, u, c, t * P:(t + 1) * P], w,
                                         start=False, stop=False)
                    last = nc.tensor.matmul(psO[:, t, :], h32[:, u, t * P:(t + 1) * P], tern32[:, :],
                                            start=False, stop=True)
                last.then_inc(down_done, 1)

            def step(s, i):
                if s == 0:
                    transposes(0, 0)
                    pe.wait_ge(prep, 9)
                    project_keys(0, 0)
                    pe.wait_ge(wsum_ready, 1)
                    nc.tensor.matmul(psQ[:, 0:2], ones[:, :], wsum[:, :], start=True,
                                     stop=True).then_inc(wsum_total, 1)
                if s + 1 < B_END:
                    transposes(s + 1, i)
                if s < A_END:
                    scores(s, i)
                    if s + 1 < A_END:
                        project_keys(s + 1, i)
                    if s == 0:
                        pe.wait_ge(prep, 10)
                    project_values(s, i)
                    if s >= 1:
                        weigh_values(s - 1, i)
                else:
                    if s == A_END:
                        pe.wait_ge(tern_step, 4)
                    if s < B_END:
                        project_up(s, i)
                    if s == A_END:
                        weigh_values(A_END - 1, 0)
                    if s > A_END:
                        sum_squares(s - 1, i)
                        project_down(s - 1, i)

            run_steps(pe, step)


def kernel(L0_attn_x, L0_attn_W, L0_attn_b, L0_ffn_w_up, L0_ffn_w_down):
    import numpy as np
    import concourse.bacc as bacc
    from concourse.bass_utils import run_bass_kernel_spmd

    x = np.ascontiguousarray(L0_attn_x)
    w = np.asarray(L0_attn_W).reshape(3, P, P)
    b = np.asarray(L0_attn_b).reshape(3, P)
    f = L0_ffn_w_up.shape[0]
    arrays = {
        "x": x,
        "w": np.ascontiguousarray(np.stack([w[0], w[1], w[2].T], axis=1)),
        "b_cols": np.ascontiguousarray(b.T),
        "b_v": np.ascontiguousarray(b[2:3]),
        "w_up_t": np.ascontiguousarray(np.asarray(L0_ffn_w_up).T),
        "w_down_t": np.ascontiguousarray(
            np.asarray(L0_ffn_w_down).T.reshape(f // P, P, P).transpose(1, 0, 2).reshape(P, f)),
    }
    nc = bacc.Bacc("TRN2", target_bir_lowering=False, num_devices=1)
    args = [nc.dram_tensor(f"in_{name}", a.shape, mybir.dt.from_np(a.dtype), kind="ExternalInput").ap()
            for name, a in arrays.items()]
    out = nc.dram_tensor("out", x.shape, F32, kind="ExternalOutput").ap()
    build(nc, *args, out)
    r = run_bass_kernel_spmd(nc, [{f"in_{name}": a for name, a in arrays.items()}], core_ids=[0])
    return r.results[0]["out"]
```

```python
from contextlib import ExitStack

import concourse.bass as bass
from concourse import mybir

P = 128
F32 = mybir.dt.float32
F16 = mybir.dt.float16
ALU = mybir.AluOpType
ACT = mybir.ActivationFunctionType
AX = mybir.AxisListType

LN_EPS = 1e-5
RMS_EPS = 1e-8

S_N = 2.0**12
S_W = 2.0**12
S_M = 2.0**8
S_P = 2.0**12
S_V = 2.0**8
S_H = 2.0**8
LN_S_P = 8.317766166719343


def build(nc, x_d, w_d, bcol_d, bv_d, wup_d, wdn_d, out_d):
    GROUPS, TOKENS, D = x_d.shape
    F = wup_d.shape[1]
    TILES = TOKENS // P
    FC = F // P
    P_SPLIT = TILES - 1
    H_SPLIT = FC - 1
    assert D == P and w_d.shape == (P, 3, D) and FC == 4 and TILES == 4 and GROUPS == 8

    x_v = x_d.rearrange("g (p t) d -> g p (t d)", t=TILES)
    out_v = out_d.rearrange("g (p t) d -> g p (t d)", t=TILES)

    with ExitStack() as ctx:
        def sb(name, shape, dt=F32):
            return ctx.enter_context(nc.sbuf_tensor(name, shape, dt))

        def psum(name, shape, dt=F32):
            return ctx.enter_context(nc.psum_tensor(name, shape, dt))

        def sem(name):
            return ctx.enter_context(nc.semaphore(name))

        x = sb("x", [P, GROUPS, TILES * D])
        w_nat = sb("w_nat", [P, 3, D])
        b_col = sb("b_col", [P, 3])
        b_v = sb("b_v", [P, D])
        bk_sel = sb("bk_sel", [P, P])
        ffn_w = sb("ffn_w", [P, 2, F])
        part = sb("part", [P, P])
        b_abs = sb("b_abs", [P, 3])
        mcol = sb("mcol", [P, 1])
        diag = sb("diag", [P, 4])
        tot = sb("tot", [P, 3])
        wsum = sb("wsum", [P, 2])
        rcp = sb("rcp", [P, 4])
        akq = sb("akq", [P, 1])
        scl = sb("scl", [P, 8])
        ident = sb("ident", [P, P])
        ones = sb("ones", [P, P])
        big = sb("big", [P, TOKENS], F16)
        m_hi = sb("m_hi", [P, P], F16)
        m_lo = sb("m_lo", [P, P], F16)
        wv_hi = sb("wv_hi", [P, P], F16)
        wv_lo = sb("wv_lo", [P, P], F16)
        c_hi = sb("c_hi", [P, P], F16)
        c_lo = sb("c_lo", [P, P], F16)
        c_mix = sb("c_mix", [P, P], F16)
        bv_hi = sb("bv_hi", [P, P], F16)
        bv_lo = sb("bv_lo", [P, P], F16)
        bv_mix = sb("bv_mix", [P, P], F16)
        t_gt = sb("t_gt", [P, 2, F], F16)
        t_lt = sb("t_lt", [P, 2, F], F16)
        tern = sb("tern", [P, 2, F], F16)
        tern32 = sb("tern32", [P, D])
        xs = sb("xs", [P, 2, TILES * D])
        bn = sb("bn", [P, 2, TILES, 6])
        mv = sb("mv", [P, 2, TILES, 2])
        nmean = sb("nmean", [P, 2, TILES])
        var2 = sb("var2", [P, 2, 2, TILES])
        root = sb("root", [P, 2, 2, TILES])
        den = sb("den", [P, 2, TILES])
        rstd = sb("rstd", [P, 2, TILES])
        p_half = sb("p_half", [P, 2, TILES])
        m_half = sb("m_half", [P, TILES])
        xn = sb("xn", [P, 2, TILES * D])
        xT_hi = sb("xT_hi", [P, 2, TOKENS], F16)
        xT_lo = sb("xT_lo", [P, 2, TOKENS], F16)
        kq_hi = sb("kq_hi", [P, TOKENS], F16)
        kq_lo = sb("kq_lo", [P, TOKENS], F16)
        nmax = sb("nmax", [P, TILES])
        nbias = sb("nbias", [P, TILES])
        prob = sb("prob", [P, P_SPLIT, TOKENS])
        prob32 = sb("prob32", [P, 2, TOKENS])
        p_hi = sb("p_hi", [P, 2, P_SPLIT, TOKENS], F16)
        p_lo = sb("p_lo", [P, 2, P_SPLIT, TOKENS], F16)
        psums = sb("psums", [P, TILES])
        rsums = sb("rsums", [P, TILES])
        v_s = sb("v_s", [P, 2, TILES, D])
        v_hi = sb("v_hi", [P, 2, P_SPLIT, D], F16)
        v_lo = sb("v_lo", [P, 2, P_SPLIT, D], F16)
        h = sb("h", [P, H_SPLIT, TOKENS])
        h32 = sb("h32", [P, 2, TOKENS])
        h_hi = sb("h_hi", [P, 2, H_SPLIT, TOKENS], F16)
        h_lo = sb("h_lo", [P, 2, H_SPLIT, TOKENS], F16)
        sq = sb("sq", [P, FC, TOKENS])
        sqs = sb("sqs", [P, 2, TOKENS])
        meansq = sb("meansq", [P, TILES])
        rms = sb("rms", [P, TILES])
        rmsd = sb("rmsd", [P, TILES])
        rrms = sb("rrms", [P, TILES])

        psT = psum("psT", [P, TOKENS])
        psV = psum("psV", [P, TILES, D])
        psS = [psum(f"psS{i}", [P, TOKENS]) for i in range(4)]
        psO = psum("psO", [P, TILES, D])
        psQ = psum("psQ", [P, TOKENS])
        psW = psQ

        w_loaded = sem("w_loaded")
        bcol_loaded = sem("bcol_loaded")
        bv_loaded = sem("bv_loaded")
        up_loaded = sem("up_loaded")
        dn_loaded = sem("dn_loaded")
        x_loaded = sem("x_loaded")
        xs_loaded = [sem("xs_loaded_even"), sem("xs_loaded_odd")]
        consts_ready = sem("consts_ready")
        ident_ready = sem("ident_ready")
        prep = sem("prep")
        pe_prep = sem("pe_prep")
        act_prep = sem("act_prep")
        rcp_ready = sem("rcp_ready")
        wsum_ready = sem("wsum_ready")
        wsum_total = sem("wsum_total")
        tern_step = sem("tern_step")
        bn_done = sem("bn_done")
        stats_ready = sem("stats_ready")
        pool_a = sem("pool_a")
        pool_b = sem("pool_b")
        rstd_done = sem("rstd_done")
        norm_stats = sem("norm_stats")
        root_ready = sem("root_ready")
        den_ready = sem("den_ready")
        rstd_ready = sem("rstd_ready")
        xn_ready = sem("xn_ready")
        xn_dve = sem("xn_dve")
        xn_half = sem("xn_half")
        t_done = sem("t_done")
        xhi_ready = sem("xhi_ready")
        xlo_ready = sem("xlo_ready")
        k_done = sem("k_done")
        kqhi_ready = sem("kqhi_ready")
        kqlo_ready = sem("kqlo_ready")
        v_done = sem("v_done")
        scores_done = sem("scores_done")
        max_done = sem("max_done")
        bias_ready = sem("bias_ready")
        exp_done = sem("exp_done")
        phi_ready = sem("phi_ready")
        plo_ready = sem("plo_ready")
        rsum_ready = sem("rsum_ready")
        vs_ready = sem("vs_ready")
        vhi_ready = sem("vhi_ready")
        vlo_ready = sem("vlo_ready")
        pv_done = sem("pv_done")
        x2_ready = sem("x2_ready")
        up_done = sem("up_done")
        gelu_done = sem("gelu_done")
        hhi_act = sem("hhi_act")
        hhi_dve = sem("hhi_dve")
        hlo_ready = sem("hlo_ready")
        sq_ready = sem("sq_ready")
        sqs_ready = sem("sqs_ready")
        q_done = sem("q_done")
        meansq_ready = sem("meansq_ready")
        rms_ready = sem("rms_ready")
        rrms_ready = sem("rrms_ready")
        down_done = sem("down_done")
        x3_ready = sem("x3_ready")
        stored = sem("stored")
        pool_gate = sem("pool_gate")
        dve_gate = sem("dve_gate")
        sp_gate = sem("sp_gate")

        EXP_SCALE, OUT_SCALE, M_SCALE, V_SCALE, T_UP, T_DN, NT_UP, NT_DN = range(8)

        A_END, B_END = GROUPS, 2 * GROUPS
        LOOPS = ((2, 6), (GROUPS + 1, GROUPS + 5))

        def after_first(g, i):
            return g >= 1 or not isinstance(i, int)

        def run_steps(eng, step):
            s = 0
            while s <= B_END:
                loop = [b for a, b in LOOPS if a == s]
                if loop:
                    with eng.Fori(0, loop[0] - s - 1, 2) as i:
                        step(s, i)
                        step(s + 1, i)
                    s = loop[0]
                else:
                    step(s, 0)
                    s += 1

        HI_ON_ACT = (0, 2)

        POOL_TILES = 2

        def h_chunk(s, c):
            return h[:, c, :] if c < H_SPLIT else h_full(s)

        assert P_SPLIT == H_SPLIT

        def h_full(s):
            return (prob32 if s == B_END - 1 else h32)[:, s % 2, :]

        def h_heads(s, c):
            return (p_hi if s == B_END - 1 else h_hi)[:, s % 2, c, :]

        def h_rests(s, c):
            return (p_lo if s == B_END - 1 else h_lo)[:, s % 2, c, :]

        def key_bank(n):
            return psO[:, :, :].rearrange("p t d -> p (t d)") if n == 0 else psT[:, :]

        block = ctx.enter_context(nc.Block())

        @block.sync
        def _(sp):
            sp.dma_start(xs[:, 0, :], x_v[0]).then_inc(xs_loaded[0], 16)
            sp.dma_start(w_nat[:, :, :], w_d).then_inc(w_loaded, 16)
            sp.dma_start(xs[:, 1, :], x_v[1]).then_inc(xs_loaded[1], 16)
            for n in (2, 3):
                sp.wait_ge(xn_ready, n - 1)
                if n == 2:
                    sp.wait_ge(xn_half, 1)
                sp.dma_start(xs[:, n % 2, :], x_v[n]).then_inc(xs_loaded[n % 2], 16)
            sp.dma_start(x[:, :, :], x_d.rearrange("g (p t) d -> p g (t d)", t=TILES)).then_inc(x_loaded, 16)
            with sp.Fori(4, GROUPS - 1, 2) as i:
                for u in range(2):
                    sp.wait_ge(xn_ready, i + u - 1)
                    sp.sem_inc(sp_gate, 1)
                    sp.dma_start(xs[:, u, :], x_v[bass.ds(i + u, 1)].rearrange("g p n -> p (g n)")
                                 ).then_inc(xs_loaded[u], 16)
            with sp.Fori(0, GROUPS - 1, 2) as i:
                for u in range(2):
                    sp.wait_ge(xn_ready, i + u + GROUPS - 1)
                    sp.sem_inc(sp_gate, 1)
                    sp.wait_ge(xn_dve, i + u + 1)
                    sp.sem_inc(sp_gate, 1)
                    sp.wait_ge(x2_ready, i + u + 1)
                    sp.sem_inc(sp_gate, 1)
                    sp.dma_start(xs[:, u, :], x[:, bass.ds(i + u, 1), :].rearrange("p g n -> p (g n)")
                                 ).then_inc(xs_loaded[u], 16)
            with sp.Fori(0, GROUPS, 1) as i:
                sp.wait_ge(x3_ready, i + 2)
                sp.dma_start(out_v[bass.ds(i, 1)].rearrange("g p n -> p g n"),
                             x[:, bass.ds(i, 1), :]).then_inc(stored, 16)
            sp.wait_ge(stored, 16 * GROUPS)

        @block.scalar
        def _(act):
            act.dma_start(b_col[:, :], bcol_d).then_inc(bcol_loaded, 16)
            act.wait_ge(consts_ready, 1)
            for row in (0, 64):
                act.dma_start(b_v[row:row + 1, :], bv_d).then_inc(bv_loaded, 16)
            act.dma_start(ffn_w[:, 0, :], wup_d).then_inc(up_loaded, 16)
            act.dma_start(ffn_w[:, 1, :], wdn_d).then_inc(dn_loaded, 16)

            act.wait_ge(prep, 8)
            nc.scalar.activation(m_hi[:, :], psS[0][:, 0:P], ACT.Identity,
                                 scale=scl[:, M_SCALE:M_SCALE + 1])
            nc.scalar.activation(c_hi[:, :], psS[0][:, P:2 * P], ACT.Identity,
                                 scale=scl[:, M_SCALE:M_SCALE + 1]).then_inc(act_prep, 1)

            def value_heads():
                act.wait_ge(bv_loaded, 32)
                nc.scalar.activation(bv_hi[:, :], b_v[:, :], ACT.Identity,
                                     scale=scl[:, V_SCALE:V_SCALE + 1])
                nc.scalar.activation(wv_hi[:, :], w_nat[:, 2, :], ACT.Identity,
                                     scale=scl[:, V_SCALE:V_SCALE + 1]).then_inc(act_prep, 1)

            def weight_sums():
                act.wait_ge(up_loaded, 16)
                nc.scalar.activation(sq[:, 0, :], ffn_w[:, 0, :], ACT.Abs, accum_out=wsum[:, 0:1])
                act.wait_ge(dn_loaded, 16)
                nc.scalar.activation(sq[:, 1, :], ffn_w[:, 1, :], ACT.Abs, accum_out=wsum[:, 1:2]).then_inc(wsum_ready, 1)

            def x_head(n, i):
                act.wait_ge(t_done, n + 1 + i)
                nc.scalar.copy(xT_hi[:, n % 2, :], psT[:, :]).then_inc(xhi_ready, 1)

            def kq_head(n, i):
                act.wait_ge(k_done, n + 1 + i)
                nc.scalar.mul(kq_hi[:, :], key_bank(n), 1.0 / (S_N * S_M)).then_inc(kqhi_ready, 1)

            def exp(s, i, j):
                act.wait_ge(bias_ready, 2 * (s + i) + j // 2 + 1)
                if s >= 1 and j < P_SPLIT:
                    act.wait_ge(plo_ready, P_SPLIT * (s - 1 + i) + j + 1)
                    if j == 0:
                        act.wait_ge(rsum_ready, s + i)
                out = prob[:, j, :] if j < P_SPLIT else prob32[:, s % 2, :]
                nc.scalar.activation(out, psS[j][:, :], ACT.Exp, bias=nbias[:, j:j + 1],
                                     scale=scl[:, EXP_SCALE:EXP_SCALE + 1],
                                     accum_out=psums[:, j:j + 1]).then_inc(exp_done, 1)

            def p_head(s, i, j):
                act.wait_ge(exp_done, 4 * (s + i) + j + 1)
                nc.scalar.copy(p_hi[:, s % 2, j, :], prob[:, j, :]).then_inc(phi_ready, 1)

            def v_head(s, i):
                act.wait_ge(vs_ready, s + 1 + i)
                nc.scalar.copy(v_hi[:, s % 2, :, :], v_s[:, s % 2, 0:P_SPLIT, :]).then_inc(vhi_ready, 1)

            def gelu(s, i, c):
                g = s - GROUPS
                act.wait_ge(up_done, 4 * (g + i) + c + 1)
                if g >= 1 and c < H_SPLIT:
                    act.wait_ge(hlo_ready, H_SPLIT * (g - 1 + i) + c + 1)
                nc.scalar.activation(h_chunk(s, c), psS[c][:, :], ACT.Gelu, scale=1.0 / S_N).then_inc(gelu_done, 1)

            def h_head_and_square(s, i, c):
                g = s - GROUPS
                act.wait_ge(gelu_done, 4 * (g + i) + c + 1)
                if c in HI_ON_ACT:
                    nc.scalar.mul(h_heads(s, c), h[:, c, :], S_H).then_inc(hhi_act, 1)
                if g >= 1 and c % 2 == 0:
                    act.wait_ge(sqs_ready, 2 * (g - 1 + i) + c // 2 + 1)
                nc.scalar.square(sq[:, c, :], h_chunk(s, c)).then_inc(sq_ready, 1)

            def step(s, i):
                if s == 0:
                    x_head(0, 0)
                    value_heads()
                    weight_sums()
                    kq_head(0, 0)
                if s == A_END:
                    v_head(s - 1, i)
                    gelu(s, i, 0)
                if s + 1 < B_END:
                    x_head(s + 1, i)
                if 1 <= s < A_END:
                    v_head(s - 1, i)
                    p_head(s - 1, i, 1)
                    p_head(s - 1, i, 2)
                if s < A_END:
                    if s <= 1:
                        kq_head(s + 1, i)
                    exp(s, i, 0)
                    exp(s, i, 1)
                    if 1 < s < A_END - 1:
                        kq_head(s + 1, i)
                    p_head(s, i, 0)
                    exp(s, i, 2)
                    exp(s, i, 3)
                    if s == A_END - 1:
                        p_head(s, i, 1)
                        p_head(s, i, 2)
                elif s < B_END:
                    if s > A_END:
                        gelu(s, i, 0)
                    for c in range(1, FC):
                        gelu(s, i, c)
                        h_head_and_square(s, i, c - 1)
                    h_head_and_square(s, i, FC - 1)

            run_steps(act, step)

        @block.gpsimd
        def _(pool):
            nc.gpsimd.memset(b_v[:, :], 0.0).then_inc(consts_ready, 1)
            nc.gpsimd.memset(p_half[:, :, :], 0.5)
            nc.gpsimd.memset(m_half[:, :], -0.5).then_inc(pool_b, 1)
            nc.gpsimd.memset(ident[:, :], 0.0).then_inc(pool_a, 1)
            pool.wait_ge(pool_a, 1)
            nc.gpsimd.affine_select(out=ident[:, :], in_=ident[:, :], compare_op=ALU.not_equal, fill=1.0,
                                    base=0, pattern=[[-1, P]], channel_multiplier=1).then_inc(ident_ready, 1)
            pool.wait_ge(pool_b, 1)

            def roots(n, i):
                u = n % 2
                pool.wait_ge(norm_stats, n + 1 + i)
                if n < GROUPS:
                    nc.gpsimd.tensor_tensor(rstd[:, u, :], var2[:, u, 1, :], m_half[:, :],
                                            ALU.pow).then_inc(rstd_done, 1)
                else:
                    nc.gpsimd.tensor_tensor(root[:, u, :, :], var2[:, u, :, :], p_half[:, :, :],
                                            ALU.pow).then_inc(root_ready, 1)

            def apply_norm(n, i):
                u = n % 2
                if n >= 2:
                    pool.wait_ge(t_done, n - 1 + i)
                if n >= GROUPS:
                    pool.wait_ge(rstd_ready, n - GROUPS + 1 + i)
                else:
                    pool.wait_ge(rstd_done, n + 1 + i)
                pool.sem_inc(pool_gate, 1)
                for t in range(TILES if n < GROUPS + 2 else POOL_TILES):
                    last = nc.gpsimd.tensor_scalar(xn[:, u, t * D:(t + 1) * D], xs[:, u, t * D:(t + 1) * D],
                                                   nmean[:, u, t:t + 1], rstd[:, u, t:t + 1], ALU.add, ALU.mult)
                last.then_inc(xn_ready, 1)

            def p_rest(s, i, j):
                pool.wait_ge(phi_ready, P_SPLIT * (s + i) + j + 1)
                nc.gpsimd.tensor_tensor(p_lo[:, s % 2, j, :], prob[:, j, :], p_hi[:, s % 2, j, :],
                                        ALU.subtract).then_inc(plo_ready, 1)

            def add_squares(s, i, k):
                g = s - GROUPS
                pool.wait_ge(sq_ready, 4 * (g + i) + 2 * k + 2)
                if g >= 1 and k == 0:
                    pool.wait_ge(q_done, g + i)
                nc.gpsimd.tensor_tensor(sqs[:, k, :], sq[:, 2 * k, :], sq[:, 2 * k + 1, :],
                                        ALU.add).then_inc(sqs_ready, 1)

            def compare_up():
                pool.wait_ge(tern_step, 1)
                nc.gpsimd.tensor_scalar(t_gt[:, 0, :], ffn_w[:, 0, :], scl[:, T_UP:T_UP + 1], None, ALU.is_gt)
                nc.gpsimd.tensor_scalar(t_lt[:, 0, :], ffn_w[:, 0, :], scl[:, NT_UP:NT_UP + 1], None,
                                        ALU.is_lt).then_inc(tern_step, 1)

            def ternary_difference():
                pool.wait_ge(tern_step, 3)
                nc.gpsimd.tensor_tensor(tern[:, :, :], t_gt[:, :, :], t_lt[:, :, :],
                                        ALU.subtract).then_inc(tern_step, 1)
                pool.wait_ge(tern_step, 4)
                nc.gpsimd.tensor_scalar(tern32[:, :], tern[:, 1, H_SPLIT * D:FC * D], S_H, 1.0,
                                        ALU.mult, ALU.mult).then_inc(tern_step, 1)

            def root_meansq(s, i):
                g = s - GROUPS
                pool.wait_ge(meansq_ready, g + 2 + i)
                nc.gpsimd.tensor_tensor(rms[:, :], meansq[:, :], p_half[:, 0, :], ALU.pow).then_inc(rms_ready, 1)

            def step(s, i):
                if s == 0:
                    roots(0, 0)
                    pool.wait_ge(rstd_done, 1)
                    for t in range(2, TILES):
                        last = nc.gpsimd.tensor_scalar(xn[:, 0, t * D:(t + 1) * D], xs[:, 0, t * D:(t + 1) * D],
                                                       nmean[:, 0, t:t + 1], rstd[:, 0, t:t + 1], ALU.add, ALU.mult)
                    last.then_inc(xn_ready, 1)
                    roots(1, 0)
                    compare_up()
                if s + 2 < B_END:
                    roots(s + 2, i)
                if s < A_END - 1:
                    if s >= 1:
                        p_rest(s - 1, i, 1)
                        p_rest(s - 1, i, 2)
                    apply_norm(s + 2, i)
                    p_rest(s, i, 0)
                    if s == 1:
                        ternary_difference()
                elif s == A_END - 1:
                    p_rest(s - 1, i, 1)
                    p_rest(s - 1, i, 2)
                    p_rest(s, i, 0)
                    apply_norm(s + 2, i)
                    p_rest(s, i, 1)
                elif s < B_END - 1:
                    if s + 2 < B_END:
                        apply_norm(s + 2, i)
                    if s > A_END:
                        root_meansq(s - 1, i)
                    add_squares(s, i, 0)
                    add_squares(s, i, 1)
                elif s == B_END - 1:
                    add_squares(s, i, 0)
                    root_meansq(s - 1, i)
                else:
                    root_meansq(s - 1, i)

            run_steps(pool, step)

        @block.vector
        def _(dve):
            def x_at(n, i):
                slot = n % GROUPS
                if isinstance(i, int):
                    return x[:, slot + i, :]
                return x[:, bass.ds(slot + i, 1), :].rearrange("p a n -> p (a n)")

            def token_stats(n, i):
                u = n % 2
                dve.wait_ge(xs_loaded[u], 16 * (n // 2) + 16 + 8 * i)
                for t in range(TILES):
                    last = nc.vector.bn_stats(bn[:, u, t, :], xs[:, u, t * D:(t + 1) * D])
                last.then_inc(bn_done, 1)

            def combine_stats(n, i):
                u = n % 2
                if n >= 2:
                    dve.wait_ge(xn_ready, n - 1 + i)
                dve.wait_ge(bn_done, n + 1 + i)
                dve.sem_inc(dve_gate, 1)
                for t in range(TILES):
                    last = nc.vector.bn_aggr(mv[:, u, t, :], bn[:, u, t, :])
                last.then_inc(stats_ready, 1)

            def norm_inputs(n, i):
                u = n % 2
                dve.wait_ge(stats_ready, n + 1 + i)
                var = mv[:, u, :, 1]
                nc.vector.tensor_scalar(nmean[:, u, :], mv[:, u, :, 0], -1.0, None, ALU.mult)
                nc.vector.tensor_scalar(var2[:, u, 0, :], var, S_N**-2, None, ALU.mult)
                nc.vector.tensor_scalar(var2[:, u, 1, :], var, LN_EPS, S_N**-2, ALU.add,
                                        ALU.mult).then_inc(norm_stats, 1)

            def apply_first(n):
                dve.wait_ge(rstd_done, n + 1)
                for t in range(2 if n == 0 else TILES):
                    last = nc.vector.tensor_scalar(xn[:, n, t * D:(t + 1) * D], xs[:, n, t * D:(t + 1) * D],
                                                   nmean[:, n, t:t + 1], rstd[:, n, t:t + 1], ALU.add, ALU.mult)
                last.then_inc(xn_ready if n else xn_half, 1)

            def x_rest(n, i):
                dve.wait_ge(xhi_ready, n + 1 + i)
                nc.vector.scalar_tensor_tensor(out=xT_lo[:, n % 2, :], in0=psT[:, :], scalar=1.0,
                                               in1=xT_hi[:, n % 2, :], op0=ALU.mult,
                                               op1=ALU.subtract).then_inc(xlo_ready, 1)

            dve.sem_inc(xn_dve, 4)
            dve.sem_inc(meansq_ready, 1)
            dve.sem_inc(rms_ready, 1)
            dve.sem_inc(x3_ready, 1)
            nc.vector.memset(part[:, :], 0.0)
            nc.vector.memset(bk_sel[:, :], 0.0)
            nc.vector.memset(ones[:, :], 1.0)
            nc.vector.memset(c_mix[:, :], 0.0)
            nc.vector.memset(bv_mix[:, :], 0.0)
            nc.vector.memset(big[:, :], S_N).then_inc(prep, 1)
            token_stats(0, 0)
            dve.wait_ge(prep, 1)
            dve.wait_ge(bcol_loaded, 16)
            nc.vector.tensor_scalar(b_abs[:, :], b_col[:, :], -1.0, None, ALU.mult)
            nc.vector.tensor_copy(bk_sel[:, 0:1], b_col[:, 1:2])
            nc.vector.tensor_copy(bk_sel[:, 64:65], b_col[:, 1:2]).then_inc(prep, 1)
            combine_stats(0, 0)
            dve.wait_ge(prep, 2)
            nc.vector.tensor_tensor(b_abs[:, :], b_abs[:, :], b_col[:, :], ALU.max)
            dve.wait_ge(w_loaded, 16)
            nc.vector.tensor_reduce(part[:, 0:3], w_nat[:, :, :], AX.X, ALU.max,
                                    apply_absolute_value=True).then_inc(prep, 1)
            norm_inputs(0, 0)
            dve.wait_ge(prep, 3)
            nc.vector.tensor_tensor(part[:, 0:3], part[:, 0:3], b_abs[:, :], ALU.max).then_inc(prep, 1)
            token_stats(1, 0)
            dve.wait_ge(pe_prep, 1)
            nc.vector.reduce_max(mcol[:, :], psW[:, 0:P], AX.X).then_inc(prep, 1)
            combine_stats(1, 0)
            dve.wait_ge(prep, 5)
            nc.vector.tensor_scalar(diag[:, 0:3], ident[:, 0:3], mcol[:, 0:1], None, ALU.mult).then_inc(prep, 1)
            norm_inputs(1, 0)
            apply_first(0)
            dve.wait_ge(pe_prep, 2)
            nc.vector.tensor_scalar(tot[:, 0:3], psW[:, P:P + 3], 1e-30, None, ALU.max).then_inc(prep, 1)
            dve.wait_ge(prep, 7)
            nc.vector.reciprocal(rcp[:, 0:3], tot[:, 0:3]).then_inc(rcp_ready, 1)
            nc.vector.tensor_scalar(scl[:, EXP_SCALE:EXP_SCALE + 1], tot[:, 0:1], tot[:, 1:2],
                                    1.0 / (D * S_N), ALU.mult, ALU.mult)
            nc.vector.tensor_scalar(scl[:, OUT_SCALE:OUT_SCALE + 1], tot[:, 2:3], 1.0 / (S_P * S_V), None,
                                    ALU.mult)
            dve.wait_ge(rcp_ready, 1)
            nc.vector.tensor_scalar(scl[:, M_SCALE:M_SCALE + 1], rcp[:, 0:1], rcp[:, 1:2], S_M, ALU.mult, ALU.mult)
            nc.vector.tensor_scalar(scl[:, V_SCALE:V_SCALE + 1], rcp[:, 2:3], S_W, None,
                                    ALU.mult).then_inc(prep, 1)
            dve.wait_ge(prep, 8)
            dve.wait_ge(act_prep, 1)
            nc.vector.scalar_tensor_tensor(out=m_lo[:, :], in0=psS[0][:, 0:P], scalar=scl[:, M_SCALE:M_SCALE + 1],
                                           in1=m_hi[:, :], op0=ALU.mult, op1=ALU.subtract)
            nc.vector.scalar_tensor_tensor(out=c_mix[64:65, :], in0=psS[0][64:65, P:2 * P],
                                           scalar=scl[64:65, M_SCALE:M_SCALE + 1],
                                           in1=c_hi[64:65, :], op0=ALU.mult, op1=ALU.subtract)
            nc.vector.tensor_copy(c_mix[0:1, :], c_hi[0:1, :]).then_inc(prep, 1)
            x_rest(0, 0)
            apply_first(1)
            dve.wait_ge(act_prep, 2)
            nc.vector.scalar_tensor_tensor(out=bv_mix[64:65, :], in0=b_v[64:65, :],
                                           scalar=scl[64:65, V_SCALE:V_SCALE + 1],
                                           in1=bv_hi[64:65, :], op0=ALU.mult, op1=ALU.subtract)
            nc.vector.tensor_copy(bv_mix[0:1, :], bv_hi[0:1, :])
            nc.vector.scalar_tensor_tensor(out=wv_lo[:, :], in0=w_nat[:, 2, :],
                                           scalar=scl[:, V_SCALE:V_SCALE + 1],
                                           in1=wv_hi[:, :], op0=ALU.mult, op1=ALU.subtract).then_inc(prep, 1)

            def thresholds():
                dve.wait_ge(wsum_total, 1)
                nc.vector.tensor_scalar(scl[:, T_UP:T_DN + 1], psQ[:, 0:2], 0.5 / (F * D), None, ALU.mult)
                nc.vector.tensor_scalar(scl[:, NT_UP:NT_DN + 1], psQ[:, 0:2], -0.5 / (F * D), None,
                                        ALU.mult).then_inc(tern_step, 1)
            def compare_down():
                dve.wait_ge(tern_step, 1)
                nc.vector.tensor_scalar(t_gt[:, 1, :], ffn_w[:, 1, :], scl[:, T_DN:T_DN + 1], None, ALU.is_gt)
                nc.vector.tensor_scalar(t_lt[:, 1, :], ffn_w[:, 1, :], scl[:, NT_DN:NT_DN + 1], None,
                                        ALU.is_lt).then_inc(tern_step, 1)

            def kq_rest(n, i):
                dve.wait_ge(kqhi_ready, n + 1 + i)
                nc.vector.scalar_tensor_tensor(out=kq_lo[:, :], in0=key_bank(n), scalar=1.0 / (S_N * S_M),
                                               in1=kq_hi[:, :], op0=ALU.mult,
                                               op1=ALU.subtract).then_inc(kqlo_ready, 1)

            def maximum(s, i, j):
                n = 4 * (s + i) + j + 1
                dve.wait_ge(scores_done, n)
                nc.vector.tensor_reduce(nmax[:, j:j + 1], psS[j][:, :], AX.X, ALU.max,
                                        negate=True).then_inc(max_done, 1)

            def exp_bias(s, i, k):
                dve.wait_ge(max_done, 4 * (s + i) + 2 * k + 2)
                nc.vector.tensor_scalar(nbias[:, 2 * k:2 * k + 2], nmax[:, 2 * k:2 * k + 2], scl[:, EXP_SCALE:EXP_SCALE + 1],
                                        LN_S_P, ALU.mult, ALU.add).then_inc(bias_ready, 1)

            def divide_values(s, i):
                dve.wait_ge(exp_done, 4 * (s + i) + 4)
                nc.vector.reciprocal(rsums[:, :], psums[:, :]).then_inc(rsum_ready, 1)
                dve.wait_ge(rsum_ready, s + 1 + i)
                dve.wait_ge(v_done, s + 1 + i)
                nc.vector.scalar_tensor_tensor(
                    out=v_s[:, s % 2, :, :], in0=psV[:, :, :], scalar=S_V * S_P / (S_N * S_W),
                    in1=rsums[:, :].unsqueeze(2).to_broadcast([P, TILES, D]),
                    op0=ALU.mult, op1=ALU.mult).then_inc(vs_ready, 1)

            def last_p_rest():
                j = P_SPLIT - 1
                u = (A_END - 1) % 2
                dve.wait_ge(phi_ready, P_SPLIT * A_END)
                nc.vector.tensor_tensor(p_lo[:, u, j, :], prob[:, j, :], p_hi[:, u, j, :],
                                        ALU.subtract).then_inc(plo_ready, 1)

            def v_rest(s, i):
                dve.wait_ge(vhi_ready, s + 1 + i)
                nc.vector.tensor_tensor(v_lo[:, s % 2, :, :], v_s[:, s % 2, 0:P_SPLIT, :], v_hi[:, s % 2, :, :],
                                        ALU.subtract).then_inc(vlo_ready, 1)

            def add_attention(s, i):
                if s == 0:
                    dve.wait_ge(x_loaded, 16)
                dve.wait_ge(pv_done, s + 1 + i)
                xg = x_at(s, i)
                nc.vector.scalar_tensor_tensor(out=xg, in0=psO[:, :, :].rearrange("p t d -> p (t d)"),
                                               scalar=scl[:, OUT_SCALE:OUT_SCALE + 1], in1=xg,
                                               op0=ALU.mult, op1=ALU.add).then_inc(x2_ready, 1)

            def norm_reciprocal(n, i):
                u = n % 2
                dve.wait_ge(root_ready, n - GROUPS + 1 + i)
                nc.vector.scalar_tensor_tensor(out=den[:, u, :], in0=root[:, u, 1, :], scalar=RMS_EPS,
                                               in1=root[:, u, 0, :], op0=ALU.mult,
                                               op1=ALU.add).then_inc(den_ready, 1)
                dve.wait_ge(den_ready, n - GROUPS + 1 + i)
                nc.vector.reciprocal(rstd[:, u, :], den[:, u, :]).then_inc(rstd_ready, 1)

            def apply_last(n, i):
                u = n % 2
                dve.wait_ge(rstd_ready, n - GROUPS + 1 + i)
                dve.wait_ge(t_done, n - 1 + i)
                for t in range(POOL_TILES, TILES):
                    last = nc.vector.tensor_scalar(xn[:, u, t * D:(t + 1) * D], xs[:, u, t * D:(t + 1) * D],
                                                   nmean[:, u, t:t + 1], rstd[:, u, t:t + 1], ALU.add, ALU.mult)
                last.then_inc(xn_dve, 1)

            def h_head(s, i, c):
                g = s - GROUPS
                dve.wait_ge(gelu_done, 4 * (g + i) + c + 1)
                nc.vector.tensor_scalar(h_heads(s, c), h[:, c, :], S_H, None, ALU.mult).then_inc(hhi_dve, 1)

            def h_rest(s, i, c):
                g = s - GROUPS
                if c in HI_ON_ACT:
                    dve.wait_ge(hhi_act, len(HI_ON_ACT) * (g + i) + HI_ON_ACT.index(c) + 1)
                else:
                    dve.wait_ge(hhi_dve, (H_SPLIT - len(HI_ON_ACT)) * (g + i) + c // 2 + 1)
                nc.vector.scalar_tensor_tensor(out=h_rests(s, c), in0=h[:, c, :], scalar=S_H,
                                               in1=h_heads(s, c), op0=ALU.mult,
                                               op1=ALU.subtract).then_inc(hlo_ready, 1)

            def last_squares():
                dve.wait_ge(sq_ready, FC * GROUPS)
                dve.wait_ge(q_done, GROUPS - 1)
                nc.vector.tensor_tensor(sqs[:, 1, :], sq[:, 2, :], sq[:, 3, :], ALU.add).then_inc(sqs_ready, 1)

            def mean_square(s, i):
                g = s - GROUPS
                dve.wait_ge(q_done, g + 1 + i)
                if after_first(g, i):
                    dve.wait_ge(rms_ready, g + i + 1)
                nc.vector.tensor_scalar(meansq[:, :], psQ[:, 0:TILES], 1.0 / F, None, ALU.mult).then_inc(meansq_ready, 1)

            def rms_reciprocal(s, i):
                g = s - GROUPS
                dve.wait_ge(rms_ready, g + 2 + i)
                nc.vector.tensor_scalar(rmsd[:, :], rms[:, :], RMS_EPS, S_H, ALU.add, ALU.mult).then_inc(rrms_ready, 1)
                dve.wait_ge(rrms_ready, 2 * (g + i) + 1)
                nc.vector.reciprocal(rrms[:, :], rmsd[:, :]).then_inc(rrms_ready, 1)

            def add_ffn(s, i):
                g = s - GROUPS
                dve.wait_ge(rrms_ready, 2 * (g + i) + 2)
                dve.wait_ge(down_done, g + 1 + i)
                xg = x_at(s, i)
                out = psV if s == B_END - 1 else psO
                for t in range(TILES):
                    last = nc.vector.scalar_tensor_tensor(
                        out=xg[:, t * D:(t + 1) * D], in0=out[:, t, :], scalar=rrms[:, t:t + 1],
                        in1=xg[:, t * D:(t + 1) * D], op0=ALU.mult, op1=ALU.add)
                last.then_inc(x3_ready, 1)

            def step(s, i):
                if s == 0:
                    thresholds()
                    kq_rest(0, 0)
                    token_stats(2, 0)
                    combine_stats(2, 0)
                    norm_inputs(2, 0)
                if s == A_END:
                    last_p_rest()
                    v_rest(A_END - 1, 0)
                if s + 1 < B_END:
                    x_rest(s + 1, i)
                if s < A_END:
                    if s >= 1:
                        v_rest(s - 1, i)
                    maximum(s, i, 0)
                    maximum(s, i, 1)
                    exp_bias(s, i, 0)
                    if s >= 2:
                        add_attention(s - 2, i)
                    maximum(s, i, 2)
                    if s + 2 >= GROUPS:
                        norm_reciprocal(s + 2, i)
                    maximum(s, i, 3)
                    exp_bias(s, i, 1)
                    if s == 0:
                        compare_down()
                        kq_rest(1, 0)
                    token_stats(s + 3, i)
                    if 1 <= s < A_END - 1:
                        kq_rest(s + 1, i)
                    combine_stats(s + 3, i)
                    norm_inputs(s + 3, i)
                    divide_values(s, i)
                elif s == A_END:
                    add_attention(A_END - 2, 0)
                    token_stats(s + 3, i)
                    norm_reciprocal(s + 2, i)
                    apply_last(s + 2, i)
                    h_rest(s, i, 0)
                    h_head(s, i, 1)
                    combine_stats(s + 3, i)
                    h_rest(s, i, 1)
                    norm_inputs(s + 3, i)
                    h_rest(s, i, 2)
                    add_attention(A_END - 1, 0)
                elif s == B_END - 1:
                    h_rest(s, i, 0)
                    h_head(s, i, 1)
                    add_ffn(s - 2, i)
                    mean_square(s - 1, i)
                    h_rest(s, i, 1)
                    h_rest(s, i, 2)
                    last_squares()
                    rms_reciprocal(s - 1, i)
                    add_ffn(s - 1, i)
                elif s < B_END:
                    if s + 3 < B_END:
                        token_stats(s + 3, i)
                    h_rest(s, i, 0)
                    h_head(s, i, 1)
                    if s + 2 < B_END:
                        norm_reciprocal(s + 2, i)
                        apply_last(s + 2, i)
                    if s + 3 < B_END:
                        combine_stats(s + 3, i)
                    mean_square(s - 1, i)
                    h_rest(s, i, 1)
                    if s + 3 < B_END:
                        norm_inputs(s + 3, i)
                    h_rest(s, i, 2)
                    rms_reciprocal(s - 1, i)
                    if s < B_END - 2:
                        add_ffn(s - 1, i)
                else:
                    mean_square(s - 1, i)
                    rms_reciprocal(s - 1, i)
                    add_ffn(s - 1, i)

            run_steps(dve, step)

        @block.tensor
        def _(pe):
            def keep_warm(n):
                for _ in range(n):
                    nc.tensor.matmul(psS[3][:, :], big[:, 0:P], big[:, :], start=True, stop=True)

            pe.wait_ge(prep, 1)
            keep_warm(8)
            pe.wait_ge(prep, 4)
            pe.wait_ge(ident_ready, 1)
            nc.tensor.transpose(psW[:, 0:P], part[:, :], ident[:, :]).then_inc(pe_prep, 1)
            nc.tensor.matmul(psS[0][:, 0:P], w_nat[:, 1, :], w_nat[:, 0, :], start=True, stop=True)
            nc.tensor.matmul(psS[0][:, P:2 * P], bk_sel[:, :], w_nat[:, 0, :], start=True, stop=True)
            keep_warm(1)
            pe.wait_ge(prep, 6)
            nc.tensor.matmul(psW[:, P:P + 3], ones[:, :], diag[:, 0:3], start=True, stop=True).then_inc(pe_prep, 1)

            def transposes(n, i):
                pe.wait_ge(xn_ready, n + 1 + i)
                if n == 0:
                    pe.wait_ge(xn_half, 1)
                if n >= GROUPS + 2:
                    pe.wait_ge(xn_dve, n - GROUPS + 3 + i)
                if n >= 1:
                    pe.wait_ge(xlo_ready, n + i)
                    if 2 <= n <= GROUPS:
                        pe.wait_ge(kqlo_ready, n + i)
                for t in range(TILES):
                    last = nc.tensor.transpose(psT[:, t * P:(t + 1) * P], xn[:, n % 2, t * D:(t + 1) * D],
                                               ident[:, :])
                last.then_inc(t_done, 1)

            def project_keys(n, i):
                pe.wait_ge(xlo_ready, n + 1 + i)
                bank = key_bank(n)
                nc.tensor.matmul(bank, m_hi[:, :], xT_hi[:, n % 2, :], start=True, stop=False)
                nc.tensor.matmul(bank, m_hi[:, :], xT_lo[:, n % 2, :], start=False, stop=False)
                nc.tensor.matmul(bank, m_lo[:, :], xT_hi[:, n % 2, :], start=False, stop=False)
                nc.tensor.matmul(bank, c_mix[:, :], big[:, :], start=False, stop=True).then_inc(k_done, 1)

            def project_values(n, i):
                if n >= 1:
                    pe.wait_ge(vs_ready, n + i)
                for t in range(TILES):
                    hi = xT_hi[:, n % 2, t * P:(t + 1) * P]
                    lo = xT_lo[:, n % 2, t * P:(t + 1) * P]
                    nc.tensor.matmul(psV[:, t, :], hi, wv_hi[:, :], start=True, stop=False)
                    nc.tensor.matmul(psV[:, t, :], hi, wv_lo[:, :], start=False, stop=False)
                    nc.tensor.matmul(psV[:, t, :], lo, wv_hi[:, :], start=False, stop=False)
                    last = nc.tensor.matmul(psV[:, t, :], big[:, 0:P], bv_mix[:, :], start=False, stop=True)
                last.then_inc(v_done, 1)

            def scores(s, i):
                pe.wait_ge(kqlo_ready, s + 1 + i)
                for j in range(TILES):
                    if s >= 1:
                        pe.wait_ge(exp_done, 4 * (s - 1 + i) + j + 1)
                    hi = kq_hi[:, j * P:(j + 1) * P]
                    lo = kq_lo[:, j * P:(j + 1) * P]
                    nc.tensor.matmul(psS[j][:, :], hi, xT_hi[:, s % 2, :], start=True, stop=False)
                    nc.tensor.matmul(psS[j][:, :], hi, xT_lo[:, s % 2, :], start=False, stop=False)
                    nc.tensor.matmul(psS[j][:, :], lo, xT_hi[:, s % 2, :], start=False,
                                     stop=True).then_inc(scores_done, 1)

            def weigh_values(s, i):
                pe.wait_ge(vlo_ready, s + 1 + i)
                pe.wait_ge(plo_ready, P_SPLIT * (s + i + 1))
                pe.wait_ge(exp_done, TILES * (s + i + 1))
                if after_first(s, i):
                    pe.wait_ge(x2_ready, s + i)
                u = s % 2
                for t in range(TILES):
                    for j in range(P_SPLIT):
                        hi = p_hi[:, u, j, t * P:(t + 1) * P]
                        lo = p_lo[:, u, j, t * P:(t + 1) * P]
                        nc.tensor.matmul(psO[:, t, :], hi, v_hi[:, u, j, :], start=(j == 0), stop=False)
                        nc.tensor.matmul(psO[:, t, :], hi, v_lo[:, u, j, :], start=False, stop=False)
                        nc.tensor.matmul(psO[:, t, :], lo, v_hi[:, u, j, :], start=False, stop=False)
                    last = nc.tensor.matmul(psO[:, t, :], prob32[:, u, t * P:(t + 1) * P], v_s[:, u, P_SPLIT, :],
                                            start=False, stop=True)
                last.then_inc(pv_done, 1)

            def project_up(s, i):
                g = s - GROUPS
                pe.wait_ge(xlo_ready, s + 1 + i)
                for c in range(FC):
                    if g >= 1:
                        pe.wait_ge(gelu_done, 4 * (g - 1 + i) + c + 1)
                    else:
                        pe.wait_ge(exp_done, 4 * (A_END - 1) + c + 1)
                    w = tern[:, 0, c * P:(c + 1) * P]
                    nc.tensor.matmul(psS[c][:, :], w, xT_hi[:, s % 2, :], start=True, stop=False)
                    nc.tensor.matmul(psS[c][:, :], w, xT_lo[:, s % 2, :], start=False,
                                     stop=True).then_inc(up_done, 1)

            def sum_squares(s, i):
                g = s - GROUPS
                pe.wait_ge(sqs_ready, 2 * (g + i) + 2)
                if after_first(g, i):
                    pe.wait_ge(meansq_ready, g + i + 1)
                for t in range(TILES):
                    nc.tensor.matmul(psQ[:, t:t + 1], sqs[:, 0, t * P:(t + 1) * P], ones[:, 0:1],
                                     start=True, stop=False)
                    last = nc.tensor.matmul(psQ[:, t:t + 1], sqs[:, 1, t * P:(t + 1) * P], ones[:, 0:1],
                                            start=False, stop=True)
                last.then_inc(q_done, 1)

            def project_down(s, i):
                g = s - GROUPS
                pe.wait_ge(hlo_ready, H_SPLIT * (g + i + 1))
                pe.wait_ge(gelu_done, FC * (g + i + 1))
                pe.wait_ge(x2_ready, GROUPS)
                out = psV if s == B_END - 1 else psO
                if after_first(g, i) and out is psO:
                    pe.wait_ge(x3_ready, g + i + 1)
                for t in range(TILES):
                    token = slice(t * P, (t + 1) * P)
                    for c in range(H_SPLIT):
                        w = tern[:, 1, c * P:(c + 1) * P]
                        nc.tensor.matmul(out[:, t, :], h_heads(s, c)[:, token], w, start=(c == 0), stop=False)
                        nc.tensor.matmul(out[:, t, :], h_rests(s, c)[:, token], w, start=False, stop=False)
                    last = nc.tensor.matmul(out[:, t, :], h_full(s)[:, token], tern32[:, :],
                                            start=False, stop=True)
                last.then_inc(down_done, 1)

            def step(s, i):
                if s == 0:
                    keep_warm(2)
                    transposes(0, 0)
                    keep_warm(6)
                    pe.wait_ge(prep, 9)
                    project_keys(0, 0)
                    pe.wait_ge(wsum_ready, 1)
                    nc.tensor.matmul(psQ[:, 0:2], ones[:, :], wsum[:, :], start=True,
                                     stop=True).then_inc(wsum_total, 1)
                if s + 1 < B_END and s != A_END:
                    transposes(s + 1, i)
                if s < A_END:
                    scores(s, i)
                    if s + 1 < A_END:
                        project_keys(s + 1, i)
                    if s == 0:
                        pe.wait_ge(prep, 10)
                    project_values(s, i)
                    if s >= 1:
                        weigh_values(s - 1, i)
                else:
                    if s == A_END:
                        pe.wait_ge(tern_step, 5)
                        project_up(s, i)
                        transposes(s + 1, i)
                        weigh_values(A_END - 1, 0)
                    elif s < B_END - 1:
                        project_up(s, i)
                    if s > A_END:
                        sum_squares(s - 1, i)
                    if s == B_END - 2:
                        project_up(s + 1, i)
                    if s > A_END:
                        project_down(s - 1, i)

            run_steps(pe, step)


def kernel(L0_attn_x, L0_attn_W, L0_attn_b, L0_ffn_w_up, L0_ffn_w_down):
    import numpy as np
    import concourse.bacc as bacc
    from concourse.bass_utils import run_bass_kernel_spmd

    x = np.ascontiguousarray(L0_attn_x)
    w = np.asarray(L0_attn_W).reshape(3, P, P)
    b = np.asarray(L0_attn_b).reshape(3, P)
    f = L0_ffn_w_up.shape[0]
    arrays = {
        "x": x,
        "w": np.ascontiguousarray(np.stack([w[0], w[1], w[2].T], axis=1)),
        "b_cols": np.ascontiguousarray(b.T),
        "b_v": np.ascontiguousarray(b[2:3]),
        "w_up_t": np.ascontiguousarray(np.asarray(L0_ffn_w_up).T),
        "w_down_t": np.ascontiguousarray(
            np.asarray(L0_ffn_w_down).T.reshape(f // P, P, P).transpose(1, 0, 2).reshape(P, f)),
    }
    nc = bacc.Bacc("TRN2", target_bir_lowering=False, num_devices=1)
    args = [nc.dram_tensor(f"in_{name}", a.shape, mybir.dt.from_np(a.dtype), kind="ExternalInput").ap()
            for name, a in arrays.items()]
    out = nc.dram_tensor("out", x.shape, F32, kind="ExternalOutput").ap()
    build(nc, *args, out)
    r = run_bass_kernel_spmd(nc, [{f"in_{name}": a for name, a in arrays.items()}], core_ids=[0])
    return r.results[0]["out"]
```
